# Optimizing a Trainium2 kernel written in Bass

```python
import numpy as np
import jax
import jax.numpy as jnp

def _softmax(x, axis=-1):
    return jax.nn.softmax(x, axis=axis)

def _gelu(x):
    return jax.nn.gelu(x, approximate=True)

def _silu(x):
    return jax.nn.silu(x)

def _sigmoid(x):
    return jax.nn.sigmoid(x)

def _layernorm(x, axis=-1, eps=1e-05):
    m = jnp.mean(x, axis=axis, keepdims=True)
    v = jnp.var(x, axis=axis, keepdims=True)
    return (x - m) / jnp.sqrt(v + eps)

def _scatter_add(tgt, idx, src, axis=0):
    return tgt.at[idx].add(src)

def _segment_sum(src, seg, n):
    return jax.ops.segment_sum(src, seg, n)
kernel_name = 'mk_macaron_d4_jaxref_r8_b52bc9'

def setup_inputs(seed: int=0):
    np.random.seed(seed)
    _w = jnp.asarray

    def _L0_attn_setup():
        import jax, jax.numpy as jnp
        import numpy as np
        import math
        D = 128
        H = 16
        DH = D // H

        def sinusoidal_pe(length, d):
            pos = jnp.arange(length, dtype=jnp.float32)[:, None]
            div = jnp.exp(jnp.arange(0, d, 2, dtype=jnp.float32) * (-math.log(10000.0) / d))
            ang = pos * div
            return jnp.stack([jnp.sin(ang), jnp.cos(ang)], axis=-1).reshape(length, d)

        def _relative_shift(pos_score):
            B, Hh, S1, S2 = pos_score.shape
            padded = jnp.concatenate([jnp.zeros((B, Hh, S1, 1), pos_score.dtype), pos_score], axis=-1)
            padded = padded.reshape(B, Hh, S2 + 1, S1)
            return padded[:, :, 1:].reshape(B, Hh, S1, S2)
        key = jax.random.key(seed)
        ks = jax.random.split(key, 12)
        s = 0.02
        x = jax.random.normal(ks[0], (2, 256, D), dtype=jnp.float32)
        return {'x': x, 'ln_g': jnp.ones((D,), jnp.float32), 'ln_b': jnp.zeros((D,), jnp.float32), 'Wq': jax.random.normal(ks[1], (D, D), jnp.float32) * s, 'bq': jnp.zeros((D,), jnp.float32), 'Wk': jax.random.normal(ks[2], (D, D), jnp.float32) * s, 'bk': jnp.zeros((D,), jnp.float32), 'Wv': jax.random.normal(ks[3], (D, D), jnp.float32) * s, 'bv': jnp.zeros((D,), jnp.float32), 'Wp': jax.random.normal(ks[4], (D, D), jnp.float32) * s, 'Wo': jax.random.normal(ks[5], (D, D), jnp.float32) * s, 'bo': jnp.zeros((D,), jnp.float32), 'u_bias': jax.random.normal(ks[6], (H, DH), jnp.float32) * 0.05, 'v_bias': jax.random.normal(ks[7], (H, DH), jnp.float32) * 0.05}
    _L0_attn_in = _L0_attn_setup()

    def _L0_ffn_setup():
        import jax, jax.numpy as jnp
        import numpy as np
        DIM = 128

        def _reference_tuple_inner(x, W_r, W_k, W_v, mu_r, mu_k):
            B, T, C = x.shape
            x_prev = jnp.concatenate([jnp.zeros((B, 1, C), x.dtype), x[:, :-1, :]], axis=1)
            xr = mu_r * x + (1.0 - mu_r) * x_prev
            xk = mu_k * x + (1.0 - mu_k) * x_prev
            r = jax.nn.sigmoid(jnp.einsum('btc,dc->btd', xr, W_r))
            k = jnp.einsum('btc,dc->btd', xk, W_k)
            k_act = jnp.square(jax.nn.relu(k))
            out = r * jnp.einsum('btc,dc->btd', k_act, W_v)
            new_state = x[:, -1, :]
            return (out, new_state)
        key = jax.random.key(seed)
        ks = jax.random.split(key, 6)
        B, T, C = (8, 256, DIM)
        x = jax.random.normal(ks[0], (B, T, C), dtype=jnp.float32)
        s = 1.0 / np.sqrt(C)
        W_r = jax.random.uniform(ks[1], (C, C), jnp.float32, -s, s)
        W_k = jax.random.uniform(ks[2], (C, C), jnp.float32, -s, s)
        W_v = jax.random.uniform(ks[3], (C, C), jnp.float32, -s, s)
        mu_r = jax.random.uniform(ks[4], (C,), jnp.float32)
        mu_k = jax.random.uniform(ks[5], (C,), jnp.float32)
        return {'x': x, 'W_r': W_r, 'W_k': W_k, 'W_v': W_v, 'mu_r': mu_r, 'mu_k': mu_k}
    _L0_ffn_in = _L0_ffn_setup()

    def _L1_attn_setup():
        import jax, jax.numpy as jnp
        import numpy as np
        import math
        B, S, E = (2, 256, 128)
        H, DK, DV = (16, 64, 64)

        def _rope(q, k):
            D = q.shape[-1]
            theta = 10000.0 ** (jnp.arange(0, D, 2, dtype=jnp.float32) / D)
            pos = jnp.arange(q.shape[-2], dtype=jnp.float32)
            freqs = pos[:, None] * (1.0 / theta)[None, :]
            emb = jnp.concatenate([freqs, freqs], axis=-1)
            cos = jnp.cos(emb)[None, None]
            sin = jnp.sin(emb)[None, None]

            def rotate(x):
                x1 = x[..., ::2]
                x2 = x[..., 1::2]
                return jnp.stack([-x2, x1], axis=-1).reshape(x.shape)
            return (q * cos + rotate(q) * sin, k * cos + rotate(k) * sin)
        key = jax.random.key(seed)
        ks = jax.random.split(key, 9)
        sE = 1.0 / math.sqrt(E)
        sV = 1.0 / math.sqrt(H * DV)
        return {'x': jax.random.normal(ks[0], (B, S, E), dtype=jnp.float32), 'wq': jax.random.uniform(ks[1], (H * DK, E), jnp.float32, -sE, sE), 'bq': jax.random.uniform(ks[2], (H * DK,), jnp.float32, -sE, sE), 'wk': jax.random.uniform(ks[3], (H * DK, E), jnp.float32, -sE, sE), 'bk': jax.random.uniform(ks[4], (H * DK,), jnp.float32, -sE, sE), 'wv': jax.random.uniform(ks[5], (H * DV, E), jnp.float32, -sE, sE), 'bv': jax.random.uniform(ks[6], (H * DV,), jnp.float32, -sE, sE), 'wo': jax.random.uniform(ks[7], (E, H * DV), jnp.float32, -sV, sV), 'bo': jax.random.uniform(ks[8], (E,), jnp.float32, -sV, sV)}
    _L1_attn_in = _L1_attn_setup()

    def _L1_ffn_setup():
        import jax, jax.numpy as jnp
        import numpy as np
        B, S, E, H, NE, TOP_K = (4, 256, 128, 256, 8, 2)
        key = jax.random.key(seed)
        ks = jax.random.split(key, 5)
        s = 0.02
        return {'x': jax.random.normal(ks[0], (B, S, E), jnp.float32), 'w1': jax.random.normal(ks[1], (NE, E, H), jnp.float32) * s, 'b1': jnp.zeros((NE, H), jnp.float32), 'w2': jax.random.normal(ks[2], (NE, H, H), jnp.float32) * s, 'b2': jnp.zeros((NE, H), jnp.float32), 'w3': jax.random.normal(ks[3], (NE, H, E), jnp.float32) * s, 'b3': jnp.zeros((NE, E), jnp.float32), 'gate_w': jax.random.normal(ks[4], (E, NE), jnp.float32) * s, 'gate_b': jnp.zeros((NE,), jnp.float32)}
    _L1_ffn_in = _L1_ffn_setup()

    def _L2_attn_setup():
        import jax, jax.numpy as jnp
        import numpy as np
        LN_EPS = 1e-05
        ATTN_EPS = 1e-05

        def _ln(x, w, b):
            mu = x.mean(-1, keepdims=True)
            var = ((x - mu) ** 2).mean(-1, keepdims=True)
            return (x - mu) * jax.lax.rsqrt(var + LN_EPS) * w + b

        def _build_mask(heads, l):
            h2 = heads // 2
            slopes = 2.0 ** jnp.linspace(0.0, -8.0, h2)
            idx = jnp.arange(l)
            decay = -jnp.maximum(idx[:, None] - idx[None, :], 0).astype(jnp.float32)
            alibi = jnp.exp(slopes[:, None, None] * decay)
            return jnp.concatenate([alibi, jnp.ones((heads - h2, l, l), dtype=jnp.float32)], axis=0)
        key = jax.random.key(seed)
        ks = jax.random.split(key, 8)
        b, l, d_model = (2, 256, 128)
        heads, exp = (16, 2)
        d_exp = d_model * exp
        d_head = d_exp // heads
        depth = 12
        f32 = jnp.float32
        inp = {'x': jax.random.normal(ks[0], (b, l, d_model), dtype=f32), 'in_ln_w': jnp.ones((d_model,), f32), 'in_ln_b': jnp.zeros((d_model,), f32), 'q_ln_w': jnp.ones((d_model,), f32), 'q_ln_b': jnp.zeros((d_model,), f32), 'k_ln_w': jnp.ones((d_model,), f32), 'k_ln_b': jnp.zeros((d_model,), f32), 'out_ln_w': jnp.ones((d_model,), f32), 'out_ln_b': jnp.zeros((d_model,), f32), 'W_in': jax.random.normal(ks[1], (d_model, 2 * d_exp), f32) * 0.02, 'W_out': jax.random.normal(ks[2], (d_exp, d_model), f32) * (0.02 / np.sqrt(2 * depth)), 'Wq': jax.random.normal(ks[3], (d_model, d_exp), f32) * 0.02, 'bq': jax.random.normal(ks[4], (d_exp,), f32) * 0.02, 'Wk': jax.random.normal(ks[5], (d_model, d_exp), f32) * 0.02, 'bk': jax.random.normal(ks[6], (d_exp,), f32) * 0.02, 'smear_factor': jnp.linspace(-6.0, 6.0, heads).astype(f32), 'log_scale': jnp.full((heads,), 0.25 * np.log(d_head), f32)}
        return inp
    _L2_attn_in = _L2_attn_setup()

    def _L2_ffn_setup():
        import jax, jax.numpy as jnp
        import numpy as np
        B, T, C = (1, 512, 128)
        E, K = (64, 8)
        G, TG = (8, 4)
        H, HS = (64, 256)
        STD = 0.02

        def _route(xf, router_w, e_bias):
            S = xf.shape[0]
            scores = jax.nn.sigmoid(xf @ router_w.T)
            sb = scores + e_bias
            epg = E // G
            grp = jax.lax.top_k(sb.reshape(S, G, epg), K // TG)[0].sum(-1)
            gidx = jax.lax.top_k(grp, TG)[1]
            gmask = jnp.zeros((S, G), bool).at[jnp.arange(S)[:, None], gidx].set(True)
            emask = jnp.repeat(gmask, epg, axis=1)
            masked = jnp.where(emask, sb, -jnp.inf)
            topk_idx = jax.lax.top_k(masked, K)[1]
            w = jnp.take_along_axis(scores, topk_idx, axis=1)
            w = w / (w.sum(-1, keepdims=True) + 1e-20)
            return (topk_idx, w)
        key = jax.random.key(seed)
        ks = jax.random.split(key, 9)
        return {'x': jax.random.normal(ks[0], (B, T, C), jnp.float32), 'router_w': jax.random.normal(ks[1], (E, C), jnp.float32) * C ** (-0.5), 'e_bias': jnp.zeros((E,), jnp.float32), 'gate_w': jax.random.normal(ks[2], (E, C, H), jnp.float32) * STD, 'up_w': jax.random.normal(ks[3], (E, C, H), jnp.float32) * STD, 'down_w': jax.random.normal(ks[4], (E, H, C), jnp.float32) * STD, 'sh_gate_w': jax.random.normal(ks[5], (C, HS), jnp.float32) * STD, 'sh_up_w': jax.random.normal(ks[6], (C, HS), jnp.float32) * STD, 'sh_down_w': jax.random.normal(ks[7], (HS, C), jnp.float32) * STD}
    _L2_ffn_in = _L2_ffn_setup()

    def _L3_attn_setup():
        import jax, jax.numpy as jnp
        import numpy as np
        ALPHA = 1.0
        N_HEADS = 16
        key = jax.random.key(seed)
        ks = jax.random.split(key, 3)
        B, N, D = (2, 256, 128)
        x = jax.random.normal(ks[0], (B, N, D), dtype=jnp.float32)
        W_qkv = jax.random.normal(ks[1], (D, 3 * D), dtype=jnp.float32) * D ** (-0.5)
        b_qkv = jnp.zeros((3 * D,), dtype=jnp.float32)
        W_proj = jax.random.normal(ks[2], (D, D), dtype=jnp.float32) * D ** (-0.5)
        b_proj = jnp.zeros((D,), dtype=jnp.float32)
        return {'x': x, 'W_qkv': W_qkv, 'b_qkv': b_qkv, 'W_proj': W_proj, 'b_proj': b_proj}
    _L3_attn_in = _L3_attn_setup()

    def _L3_ffn_setup():
        import jax, jax.numpy as jnp
        import numpy as np
        EPS = 1e-05
        LN_EPS = 1e-05
        NUM_EXPERTS = 8
        TOP_K = 2
        HIDDEN = 128
        INTER = 256

        def _swiglu(x, wg, wu, wd):
            return jax.nn.silu(x @ wg) * (x @ wu) @ wd
        key = jax.random.key(seed)
        ks = jax.random.split(key, 10)
        B, S, H, I, E = (8, 512, HIDDEN, INTER, NUM_EXPERTS)
        std_h = 1.0 / np.sqrt(H)
        std_i = 1.0 / np.sqrt(I)
        return {'x': jax.random.normal(ks[0], (B, S, H), dtype=jnp.float32), 'ln_scale': jnp.ones((H,), dtype=jnp.float32), 'ln_bias': jnp.zeros((H,), dtype=jnp.float32), 'gate_w': jax.random.normal(ks[1], (E, H), dtype=jnp.float32) * 0.01, 'Wg': jax.random.normal(ks[2], (E, H, I), dtype=jnp.float32) * std_h, 'Wu': jax.random.normal(ks[3], (E, H, I), dtype=jnp.float32) * std_h, 'Wd': jax.random.normal(ks[4], (E, I, H), dtype=jnp.float32) * std_i, 'sWg': jax.random.normal(ks[5], (H, I), dtype=jnp.float32) * std_h, 'sWu': jax.random.normal(ks[6], (H, I), dtype=jnp.float32) * std_h, 'sWd': jax.random.normal(ks[7], (I, H), dtype=jnp.float32) * std_i}
    _L3_ffn_in = _L3_ffn_setup()
    _d = {'L0_attn_x': _L0_attn_in['x'], 'L0_attn_ln_g': _L0_attn_in['ln_g'], 'L0_attn_ln_b': _L0_attn_in['ln_b'], 'L0_attn_Wq': _L0_attn_in['Wq'], 'L0_attn_bq': _L0_attn_in['bq'], 'L0_attn_Wk': _L0_attn_in['Wk'], 'L0_attn_bk': _L0_attn_in['bk'], 'L0_attn_Wv': _L0_attn_in['Wv'], 'L0_attn_bv': _L0_attn_in['bv'], 'L0_attn_Wp': _L0_attn_in['Wp'], 'L0_attn_Wo': _L0_attn_in['Wo'], 'L0_attn_bo': _L0_attn_in['bo'], 'L0_attn_u_bias': _L0_attn_in['u_bias'], 'L0_attn_v_bias': _L0_attn_in['v_bias'], 'L0_ffn_W_r': _L0_ffn_in['W_r'], 'L0_ffn_W_k': _L0_ffn_in['W_k'], 'L0_ffn_W_v': _L0_ffn_in['W_v'], 'L0_ffn_mu_r': _L0_ffn_in['mu_r'], 'L0_ffn_mu_k': _L0_ffn_in['mu_k'], 'L1_attn_wq': _L1_attn_in['wq'], 'L1_attn_bq': _L1_attn_in['bq'], 'L1_attn_wk': _L1_attn_in['wk'], 'L1_attn_bk': _L1_attn_in['bk'], 'L1_attn_wv': _L1_attn_in['wv'], 'L1_attn_bv': _L1_attn_in['bv'], 'L1_attn_wo': _L1_attn_in['wo'], 'L1_attn_bo': _L1_attn_in['bo'], 'L1_ffn_w1': _L1_ffn_in['w1'], 'L1_ffn_b1': _L1_ffn_in['b1'], 'L1_ffn_w2': _L1_ffn_in['w2'], 'L1_ffn_b2': _L1_ffn_in['b2'], 'L1_ffn_w3': _L1_ffn_in['w3'], 'L1_ffn_b3': _L1_ffn_in['b3'], 'L1_ffn_gate_w': _L1_ffn_in['gate_w'], 'L1_ffn_gate_b': _L1_ffn_in['gate_b'], 'L2_attn_in_ln_w': _L2_attn_in['in_ln_w'], 'L2_attn_in_ln_b': _L2_attn_in['in_ln_b'], 'L2_attn_q_ln_w': _L2_attn_in['q_ln_w'], 'L2_attn_q_ln_b': _L2_attn_in['q_ln_b'], 'L2_attn_k_ln_w': _L2_attn_in['k_ln_w'], 'L2_attn_k_ln_b': _L2_attn_in['k_ln_b'], 'L2_attn_out_ln_w': _L2_attn_in['out_ln_w'], 'L2_attn_out_ln_b': _L2_attn_in['out_ln_b'], 'L2_attn_W_in': _L2_attn_in['W_in'], 'L2_attn_W_out': _L2_attn_in['W_out'], 'L2_attn_Wq': _L2_attn_in['Wq'], 'L2_attn_bq': _L2_attn_in['bq'], 'L2_attn_Wk': _L2_attn_in['Wk'], 'L2_attn_bk': _L2_attn_in['bk'], 'L2_attn_smear_factor': _L2_attn_in['smear_factor'], 'L2_attn_log_scale': _L2_attn_in['log_scale'], 'L2_ffn_router_w': _L2_ffn_in['router_w'], 'L2_ffn_e_bias': _L2_ffn_in['e_bias'], 'L2_ffn_gate_w': _L2_ffn_in['gate_w'], 'L2_ffn_up_w': _L2_ffn_in['up_w'], 'L2_ffn_down_w': _L2_ffn_in['down_w'], 'L2_ffn_sh_gate_w': _L2_ffn_in['sh_gate_w'], 'L2_ffn_sh_up_w': _L2_ffn_in['sh_up_w'], 'L2_ffn_sh_down_w': _L2_ffn_in['sh_down_w'], 'L3_attn_W_qkv': _L3_attn_in['W_qkv'], 'L3_attn_b_qkv': _L3_attn_in['b_qkv'], 'L3_attn_W_proj': _L3_attn_in['W_proj'], 'L3_attn_b_proj': _L3_attn_in['b_proj'], 'L3_ffn_ln_scale': _L3_ffn_in['ln_scale'], 'L3_ffn_ln_bias': _L3_ffn_in['ln_bias'], 'L3_ffn_gate_w': _L3_ffn_in['gate_w'], 'L3_ffn_Wg': _L3_ffn_in['Wg'], 'L3_ffn_Wu': _L3_ffn_in['Wu'], 'L3_ffn_Wd': _L3_ffn_in['Wd'], 'L3_ffn_sWg': _L3_ffn_in['sWg'], 'L3_ffn_sWu': _L3_ffn_in['sWu'], 'L3_ffn_sWd': _L3_ffn_in['sWd']}
    _x0 = _d['L0_attn_x']
    _d['L0_attn_x'] = jax.random.normal(jax.random.fold_in(jax.random.key(seed), 1), (4, 512, 128), dtype=_x0.dtype)
    del _x0
    return _d

def reference(L0_attn_x, L0_attn_ln_g, L0_attn_ln_b, L0_attn_Wq, L0_attn_bq, L0_attn_Wk, L0_attn_bk, L0_attn_Wv, L0_attn_bv, L0_attn_Wp, L0_attn_Wo, L0_attn_bo, L0_attn_u_bias, L0_attn_v_bias, L0_ffn_W_r, L0_ffn_W_k, L0_ffn_W_v, L0_ffn_mu_r, L0_ffn_mu_k, L1_attn_wq, L1_attn_bq, L1_attn_wk, L1_attn_bk, L1_attn_wv, L1_attn_bv, L1_attn_wo, L1_attn_bo, L1_ffn_w1, L1_ffn_b1, L1_ffn_w2, L1_ffn_b2, L1_ffn_w3, L1_ffn_b3, L1_ffn_gate_w, L1_ffn_gate_b, L2_attn_in_ln_w, L2_attn_in_ln_b, L2_attn_q_ln_w, L2_attn_q_ln_b, L2_attn_k_ln_w, L2_attn_k_ln_b, L2_attn_out_ln_w, L2_attn_out_ln_b, L2_attn_W_in, L2_attn_W_out, L2_attn_Wq, L2_attn_bq, L2_attn_Wk, L2_attn_bk, L2_attn_smear_factor, L2_attn_log_scale, L2_ffn_router_w, L2_ffn_e_bias, L2_ffn_gate_w, L2_ffn_up_w, L2_ffn_down_w, L2_ffn_sh_gate_w, L2_ffn_sh_up_w, L2_ffn_sh_down_w, L3_attn_W_qkv, L3_attn_b_qkv, L3_attn_W_proj, L3_attn_b_proj, L3_ffn_ln_scale, L3_ffn_ln_bias, L3_ffn_gate_w, L3_ffn_Wg, L3_ffn_Wu, L3_ffn_Wd, L3_ffn_sWg, L3_ffn_sWu, L3_ffn_sWd):

    def _L0_attn_ref(x, ln_g, ln_b, Wq, bq, Wk, bk, Wv, bv, Wp, Wo, bo, u_bias, v_bias):
        import jax, jax.numpy as jnp
        import numpy as np
        import math
        D = 128
        H = 16
        DH = D // H

        def sinusoidal_pe(length, d):
            pos = jnp.arange(length, dtype=jnp.float32)[:, None]
            div = jnp.exp(jnp.arange(0, d, 2, dtype=jnp.float32) * (-math.log(10000.0) / d))
            ang = pos * div
            return jnp.stack([jnp.sin(ang), jnp.cos(ang)], axis=-1).reshape(length, d)

        def _relative_shift(pos_score):
            B, Hh, S1, S2 = pos_score.shape
            padded = jnp.concatenate([jnp.zeros((B, Hh, S1, 1), pos_score.dtype), pos_score], axis=-1)
            padded = padded.reshape(B, Hh, S2 + 1, S1)
            return padded[:, :, 1:].reshape(B, Hh, S1, S2)
        B, S, Dm = x.shape
        dh = Dm // H
        scale = dh ** (-0.5)
        pe = sinusoidal_pe(S, Dm)
        mu = jnp.mean(x, axis=-1, keepdims=True)
        var = jnp.var(x, axis=-1, keepdims=True)
        xn = (x - mu) / jnp.sqrt(var + 1e-05) * ln_g + ln_b
        q = (xn @ Wq + bq).reshape(B, S, H, dh)
        k = (xn @ Wk + bk).reshape(B, S, H, dh)
        v = (xn @ Wv + bv).reshape(B, S, H, dh)
        p = (pe @ Wp).reshape(S, H, dh)
        content = jnp.einsum('bihd,bjhd->bhij', q + u_bias, k)
        pos = jnp.einsum('bihd,jhd->bhij', q + v_bias, p)
        pos = _relative_shift(pos)
        attn = jax.nn.softmax((content + pos) * scale, axis=-1)
        head = jnp.einsum('bhij,bjhd->bihd', attn, v).reshape(B, S, Dm)
        return head @ Wo + bo

    def _L0_ffn_ref(x, W_r, W_k, W_v, mu_r, mu_k):
        import jax, jax.numpy as jnp
        import numpy as np
        DIM = 128

        def _reference_tuple_inner(x, W_r, W_k, W_v, mu_r, mu_k):
            B, T, C = x.shape
            x_prev = jnp.concatenate([jnp.zeros((B, 1, C), x.dtype), x[:, :-1, :]], axis=1)
            xr = mu_r * x + (1.0 - mu_r) * x_prev
            xk = mu_k * x + (1.0 - mu_k) * x_prev
            r = jax.nn.sigmoid(jnp.einsum('btc,dc->btd', xr, W_r))
            k = jnp.einsum('btc,dc->btd', xk, W_k)
            k_act = jnp.square(jax.nn.relu(k))
            out = r * jnp.einsum('btc,dc->btd', k_act, W_v)
            new_state = x[:, -1, :]
            return (out, new_state)
        return _reference_tuple_inner(x, W_r, W_k, W_v, mu_r, mu_k)[0]

    def _L1_attn_ref(x, wq, bq, wk, bk, wv, bv, wo, bo):
        import jax, jax.numpy as jnp
        import numpy as np
        import math
        B, S, E = (2, 256, 128)
        H, DK, DV = (16, 64, 64)

        def _rope(q, k):
            D = q.shape[-1]
            theta = 10000.0 ** (jnp.arange(0, D, 2, dtype=jnp.float32) / D)
            pos = jnp.arange(q.shape[-2], dtype=jnp.float32)
            freqs = pos[:, None] * (1.0 / theta)[None, :]
            emb = jnp.concatenate([freqs, freqs], axis=-1)
            cos = jnp.cos(emb)[None, None]
            sin = jnp.sin(emb)[None, None]

            def rotate(x):
                x1 = x[..., ::2]
                x2 = x[..., 1::2]
                return jnp.stack([-x2, x1], axis=-1).reshape(x.shape)
            return (q * cos + rotate(q) * sin, k * cos + rotate(k) * sin)
        Bx, Sx, Ex = x.shape
        q = (x @ wq.T + bq).reshape(Bx, Sx, H, DK).transpose(0, 2, 1, 3)
        k = (x @ wk.T + bk).reshape(Bx, Sx, H, DK).transpose(0, 2, 1, 3)
        v = (x @ wv.T + bv).reshape(Bx, Sx, H, DV).transpose(0, 2, 1, 3)
        q, k = _rope(q, k)
        scores = jnp.einsum('bhqd,bhkd->bhqk', q, k)
        causal = jnp.triu(jnp.ones((Sx, Sx), dtype=bool), k=1)
        scores = jnp.where(causal[None, None], -jnp.inf, scores)
        attn = jax.nn.softmax(scores / math.sqrt(DK), axis=-1)
        out = jnp.einsum('bhqk,bhkd->bhqd', attn, v)
        out = out.transpose(0, 2, 1, 3).reshape(Bx, Sx, H * DV)
        return out @ wo.T + bo

    def _L1_ffn_ref(x, w1, b1, w2, b2, w3, b3, gate_w, gate_b):
        import jax, jax.numpy as jnp
        import numpy as np
        B, S, E, H, NE, TOP_K = (4, 256, 128, 256, 8, 2)
        gate_weights = jax.nn.softmax(x @ gate_w + gate_b, axis=-1)
        topk_vals, topk_idx = jax.lax.top_k(gate_weights, TOP_K)
        h = jax.nn.gelu(jnp.einsum('bse,neh->bsnh', x, w1) + b1, approximate=False)
        h = jax.nn.gelu(jnp.einsum('bsnh,nhk->bsnk', h, w2) + b2, approximate=False)
        expert_out = jnp.einsum('bsnh,nhe->bsne', h, w3) + b3
        gathered = jnp.take_along_axis(expert_out, topk_idx[..., None], axis=2)
        return jnp.sum(topk_vals[..., None] * gathered, axis=2)

    def _L2_attn_ref(x, in_ln_w, in_ln_b, q_ln_w, q_ln_b, k_ln_w, k_ln_b, out_ln_w, out_ln_b, W_in, W_out, Wq, bq, Wk, bk, smear_factor, log_scale):
        import jax, jax.numpy as jnp
        import numpy as np
        LN_EPS = 1e-05
        ATTN_EPS = 1e-05

        def _ln(x, w, b):
            mu = x.mean(-1, keepdims=True)
            var = ((x - mu) ** 2).mean(-1, keepdims=True)
            return (x - mu) * jax.lax.rsqrt(var + LN_EPS) * w + b

        def _build_mask(heads, l):
            h2 = heads // 2
            slopes = 2.0 ** jnp.linspace(0.0, -8.0, h2)
            idx = jnp.arange(l)
            decay = -jnp.maximum(idx[:, None] - idx[None, :], 0).astype(jnp.float32)
            alibi = jnp.exp(slopes[:, None, None] * decay)
            return jnp.concatenate([alibi, jnp.ones((heads - h2, l, l), dtype=jnp.float32)], axis=0)
        b, l, d_model = x.shape
        heads = smear_factor.shape[0]
        d_exp = W_in.shape[1] // 2
        d_head = d_exp // heads
        vp = _ln(x, in_ln_w, in_ln_b) @ W_in
        v, p = jnp.split(vp, 2, axis=-1)
        q = _ln(x, q_ln_w, q_ln_b) @ Wq + bq
        k = _ln(x, k_ln_w, k_ln_b) @ Wk + bk

        def to_heads(t):
            return t.reshape(b, l, heads, d_head).transpose(0, 2, 1, 3)
        q, k, v = (to_heads(q), to_heads(k), to_heads(v))
        q = jax.nn.softmax(q, axis=-1)
        k = jax.nn.softmax(k, axis=-1)
        smear = jax.nn.sigmoid(smear_factor)[None, :, None, None]
        k_prev = jnp.pad(k, ((0, 0), (0, 0), (1, 0), (0, 0)))[:, :, :l, :]
        k = (1.0 - smear) * k + smear * k_prev
        s = jnp.exp(log_scale)[None, :, None, None]
        q = q / s
        k = k / s
        mask = _build_mask(heads, l)
        attn = jnp.tril(jnp.einsum('bhid,bhjd->bhij', q, k) * mask)
        norm = 1.0 / (attn.sum(axis=-1) + ATTN_EPS)
        o = jnp.einsum('bhij,bhjd->bhid', attn * norm[..., None], v)
        o = o.transpose(0, 2, 1, 3).reshape(b, l, d_exp)
        out = _ln(jax.nn.silu(p) * o @ W_out, out_ln_w, out_ln_b)
        return out

    def _L2_ffn_ref(x, router_w, e_bias, gate_w, up_w, down_w, sh_gate_w, sh_up_w, sh_down_w):
        import jax, jax.numpy as jnp
        import numpy as np
        B, T, C = (1, 512, 128)
        E, K = (64, 8)
        G, TG = (8, 4)
        H, HS = (64, 256)
        STD = 0.02

        def _route(xf, router_w, e_bias):
            S = xf.shape[0]
            scores = jax.nn.sigmoid(xf @ router_w.T)
            sb = scores + e_bias
            epg = E // G
            grp = jax.lax.top_k(sb.reshape(S, G, epg), K // TG)[0].sum(-1)
            gidx = jax.lax.top_k(grp, TG)[1]
            gmask = jnp.zeros((S, G), bool).at[jnp.arange(S)[:, None], gidx].set(True)
            emask = jnp.repeat(gmask, epg, axis=1)
            masked = jnp.where(emask, sb, -jnp.inf)
            topk_idx = jax.lax.top_k(masked, K)[1]
            w = jnp.take_along_axis(scores, topk_idx, axis=1)
            w = w / (w.sum(-1, keepdims=True) + 1e-20)
            return (topk_idx, w)
        Bq, Tq, Cq = x.shape
        xf = x.reshape(Bq * Tq, Cq)
        shared = jax.nn.silu(xf @ sh_gate_w) * (xf @ sh_up_w) @ sh_down_w
        topk_idx, w = _route(xf, router_w, e_bias)
        fe = topk_idx.reshape(-1)
        order = jnp.argsort(fe, stable=True)
        tok = order // K
        sorted_x = xf[tok]
        group_sizes = jnp.bincount(fe, length=E).astype(jnp.int32)
        g = jax.lax.ragged_dot(sorted_x, gate_w, group_sizes)
        u = jax.lax.ragged_dot(sorted_x, up_w, group_sizes)
        h = jax.nn.silu(g) * u
        o = jax.lax.ragged_dot(h, down_w, group_sizes)
        o = o * w.reshape(-1)[order][:, None]
        routed = jnp.zeros_like(xf).at[tok].add(o)
        return (shared + routed).reshape(Bq, Tq, Cq)

    def _L3_attn_ref(x, W_qkv, b_qkv, W_proj, b_proj):
        import jax, jax.numpy as jnp
        import numpy as np
        ALPHA = 1.0
        N_HEADS = 16
        B, N, D = x.shape
        H = N_HEADS
        hd = D // H
        qkv = (x @ W_qkv + b_qkv).reshape(B, N, 3, H, hd).transpose(2, 0, 3, 1, 4)
        q, k, v = (qkv[0], qkv[1], qkv[2])
        q_row_2 = jnp.max(jnp.sum(jnp.abs(q), axis=-1), axis=-1) ** 2
        k_col_2 = jnp.max(jnp.sum(jnp.abs(k), axis=-2), axis=-1) ** 2
        fro_q = jnp.sqrt(jnp.sum(q * q, axis=(-2, -1)))
        inf_xt = jnp.max(jnp.sum(jnp.abs(x), axis=-2), axis=-1)
        denom = fro_q * inf_xt[:, None]
        qk = jnp.einsum('bhnd,bhmd->bhnm', q, k)
        sim = -ALPHA * (q_row_2[:, :, None, None] - 2.0 * qk + k_col_2[:, :, None, None]) / denom[:, :, None, None]
        attn = jax.nn.softmax(sim, axis=-1)
        weighted = jnp.einsum('bhnm,bhmd->bhnd', attn, v)
        weighted = weighted.transpose(0, 2, 1, 3).reshape(B, N, D)
        return weighted @ W_proj + b_proj

    def _L3_ffn_ref(x, ln_scale, ln_bias, gate_w, Wg, Wu, Wd, sWg, sWu, sWd):
        import jax, jax.numpy as jnp
        import numpy as np
        EPS = 1e-05
        LN_EPS = 1e-05
        NUM_EXPERTS = 8
        TOP_K = 2
        HIDDEN = 128
        INTER = 256

        def _swiglu(x, wg, wu, wd):
            return jax.nn.silu(x @ wg) * (x @ wu) @ wd
        B, S, H = x.shape
        xf = x.reshape(-1, H)
        mu = jnp.mean(xf, axis=-1, keepdims=True)
        var = jnp.var(xf, axis=-1, keepdims=True)
        xn = (xf - mu) * jax.lax.rsqrt(var + LN_EPS) * ln_scale + ln_bias
        logits = xn @ gate_w.T
        probs = jax.nn.softmax(logits, axis=-1)
        tk_probs, tk_idx = jax.lax.top_k(probs, TOP_K)
        tk_probs = tk_probs / (jnp.sum(tk_probs, axis=-1, keepdims=True) + EPS)
        onehot = tk_idx[..., None] == jnp.arange(NUM_EXPERTS)[None, None, :]
        w = jnp.sum(tk_probs[..., None] * onehot.astype(tk_probs.dtype), axis=1)
        out = _swiglu(xf, sWg, sWu, sWd)
        for e in range(NUM_EXPERTS):
            out = out + w[:, e:e + 1] * _swiglu(xf, Wg[e], Wu[e], Wd[e])
        return out.reshape(B, S, H)
    x = L0_attn_x
    x = x + 0.5 * _L0_ffn_ref(_layernorm(x, axis=-1), L0_ffn_W_r, L0_ffn_W_k, L0_ffn_W_v, L0_ffn_mu_r, L0_ffn_mu_k)
    x = x + _L0_attn_ref(_layernorm(x, axis=-1), L0_attn_ln_g, L0_attn_ln_b, L0_attn_Wq, L0_attn_bq, L0_attn_Wk, L0_attn_bk, L0_attn_Wv, L0_attn_bv, L0_attn_Wp, L0_attn_Wo, L0_attn_bo, L0_attn_u_bias, L0_attn_v_bias)
    x = x + 0.5 * _L0_ffn_ref(_layernorm(x, axis=-1), L0_ffn_W_r, L0_ffn_W_k, L0_ffn_W_v, L0_ffn_mu_r, L0_ffn_mu_k)
    x = x + 0.5 * _L1_ffn_ref(_layernorm(x, axis=-1), L1_ffn_w1, L1_ffn_b1, L1_ffn_w2, L1_ffn_b2, L1_ffn_w3, L1_ffn_b3, L1_ffn_gate_w, L1_ffn_gate_b)
    x = x + _L1_attn_ref(_layernorm(x, axis=-1), L1_attn_wq, L1_attn_bq, L1_attn_wk, L1_attn_bk, L1_attn_wv, L1_attn_bv, L1_attn_wo, L1_attn_bo)
    x = x + 0.5 * _L1_ffn_ref(_layernorm(x, axis=-1), L1_ffn_w1, L1_ffn_b1, L1_ffn_w2, L1_ffn_b2, L1_ffn_w3, L1_ffn_b3, L1_ffn_gate_w, L1_ffn_gate_b)
    x = x + 0.5 * _L2_ffn_ref(_layernorm(x, axis=-1), L2_ffn_router_w, L2_ffn_e_bias, L2_ffn_gate_w, L2_ffn_up_w, L2_ffn_down_w, L2_ffn_sh_gate_w, L2_ffn_sh_up_w, L2_ffn_sh_down_w)
    x = x + _L2_attn_ref(_layernorm(x, axis=-1), L2_attn_in_ln_w, L2_attn_in_ln_b, L2_attn_q_ln_w, L2_attn_q_ln_b, L2_attn_k_ln_w, L2_attn_k_ln_b, L2_attn_out_ln_w, L2_attn_out_ln_b, L2_attn_W_in, L2_attn_W_out, L2_attn_Wq, L2_attn_bq, L2_attn_Wk, L2_attn_bk, L2_attn_smear_factor, L2_attn_log_scale)
    x = x + 0.5 * _L2_ffn_ref(_layernorm(x, axis=-1), L2_ffn_router_w, L2_ffn_e_bias, L2_ffn_gate_w, L2_ffn_up_w, L2_ffn_down_w, L2_ffn_sh_gate_w, L2_ffn_sh_up_w, L2_ffn_sh_down_w)
    x = x + 0.5 * _L3_ffn_ref(_layernorm(x, axis=-1), L3_ffn_ln_scale, L3_ffn_ln_bias, L3_ffn_gate_w, L3_ffn_Wg, L3_ffn_Wu, L3_ffn_Wd, L3_ffn_sWg, L3_ffn_sWu, L3_ffn_sWd)
    x = x + _L3_attn_ref(_layernorm(x, axis=-1), L3_attn_W_qkv, L3_attn_b_qkv, L3_attn_W_proj, L3_attn_b_proj)
    x = x + 0.5 * _L3_ffn_ref(_layernorm(x, axis=-1), L3_ffn_ln_scale, L3_ffn_ln_bias, L3_ffn_gate_w, L3_ffn_Wg, L3_ffn_Wu, L3_ffn_Wd, L3_ffn_sWg, L3_ffn_sWu, L3_ffn_sWd)
    return x

_drawn_inputs = setup_inputs


def setup_inputs(seed=0):
    import zlib

    import numpy as np

    out = dict(_drawn_inputs(seed))
    spreads = {'L0_attn_ln_g': (1.0, 0.6),
     'L0_attn_ln_b': (0.0, 0.351),
     'L0_attn_bq': (0.0, 0.8),
     'L0_attn_bk': (0.0, 2.0),
     'L0_attn_bv': (0.0, 0.1),
     'L0_attn_bo': (0.0, 0.1),
     'L1_ffn_b1': (0.0, 0.8),
     'L1_ffn_b2': (0.0, 0.443),
     'L1_ffn_b3': (0.0, 0.1),
     'L1_ffn_gate_b': (0.0, 0.27),
     'L2_attn_in_ln_w': (1.0, 0.2),
     'L2_attn_in_ln_b': (0.0, 0.1),
     'L2_attn_q_ln_w': (1.0, 0.6),
     'L2_attn_q_ln_b': (0.0, 0.8),
     'L2_attn_k_ln_w': (1.0, 0.6),
     'L2_attn_k_ln_b': (0.0, 0.8),
     'L2_attn_out_ln_w': (1.0, 0.2),
     'L2_attn_out_ln_b': (0.0, 0.1),
     'L2_attn_log_scale': (0.6931471824645996, 0.6),
     'L2_ffn_e_bias': (0.0, 0.8),
     'L3_attn_b_qkv': (0.0, 0.1),
     'L3_attn_b_proj': (0.0, 0.1),
     'L3_ffn_ln_scale': (1.0, 0.2),
     'L3_ffn_ln_bias': (0.0, 0.1)}
    factors = {'L0_attn_Wq': 8.0,
     'L0_attn_Wk': 8.0,
     'L0_attn_Wp': 8.0,
     'L0_attn_u_bias': 8.0,
     'L0_attn_v_bias': 8.0,
     'L1_attn_bq': 5.921,
     'L1_attn_bk': 8.0,
     'L1_ffn_w1': 7.95,
     'L1_ffn_w2': 6.182,
     'L1_ffn_w3': 3.654,
     'L2_attn_Wq': 7.874,
     'L2_attn_bq': 8.0,
     'L2_attn_Wk': 6.569,
     'L2_attn_bk': 8.0,
     'L2_attn_smear_factor': 3.188,
     'L2_ffn_router_w': 8.0,
     'L2_ffn_gate_w': 6.211,
     'L2_ffn_up_w': 6.783,
     'L2_ffn_down_w': 6.576,
     'L2_ffn_sh_gate_w': 2.953,
     'L2_ffn_sh_up_w': 2.775,
     'L2_ffn_sh_down_w': 2.826}
    for name, (base, spread) in spreads.items():
        noise = np.random.default_rng([zlib.crc32(name.encode()), seed]).standard_normal(out[name].shape)
        drawn = base * np.exp(spread * noise) if base else spread * noise
        out[name] = jnp.asarray(drawn.astype(out[name].dtype))
    for name, factor in factors.items():
        out[name] = (out[name] * factor).astype(out[name].dtype)
    return out
```

```python
from collections import namedtuple
from contextlib import ExitStack

import numpy as np

import concourse.bass as bass
from concourse import mybir

F32 = mybir.dt.float32
BF16 = mybir.dt.bfloat16
F32R = mybir.dt.float32r
I32 = mybir.dt.int32
ALU = mybir.AluOpType
ACT = mybir.ActivationFunctionType
AX = mybir.AxisListType
ds = bass.ds

P = 128
B = 4
S = 512
TB = S // P
NT = B * TB
T = B * S
H = 16
HID = 256
NE = 8
E2 = 64
H2 = 64
G2 = 8
PAIRS = 2 + E2 // 2
LN_EPS = 1e-5
BIG = 1e30
PRIME = 16

COLS = ["mu_r", "mu_k", "l0_g", "l0_b", "l0_bq", "l0_bk", "l0_u", "l0_v",
        "in_w", "in_b", "q_w", "q_b", "k_w", "k_b", "smear0", "smear1", "ls0", "ls1",
        "l3_bq", "l3_bk", "l3_s", "l3_b"]
MATS = ["ident", "Wr", "Wk", "Wv", "aq", "ak", "av", "ap", "ao", "pq", "pk", "pv", "po", "wo0", "wo1"]
ROWS = [("ones", P), ("l0_bv", P), ("l0_bo", P), ("l1_bv", H * 64), ("l1_bo", P), ("l2_bq", 256),
        ("l2_bk", 256), ("l3_bv", P), ("l3_bo", P)]
CONSTS = 16 * 6
NMASK = H + 2


class Chain:

    def __init__(self, eng, sem):
        self.eng, self.sem, self.n = eng, sem, 0

    def link(self, ins):
        self.n += 1
        ins.then_inc(self.sem, 1)
        self.eng.wait_ge(self.sem, self.n)


UPPER = -4096


def split(eng, link, x, tmp, hi, lo):
    link(eng.tensor_scalar(tmp.bitcast(I32), x.bitcast(I32), UPPER, None, ALU.bitwise_and))
    eng.tensor_copy(hi, tmp)
    return eng.tensor_tensor(lo, x, tmp, ALU.subtract)


def product(pe, out, w, x):
    (wh, wl), (xh, xl) = w, x
    pe.matmul(out, wh, xh, start=True, stop=False)
    pe.matmul(out, wh, xl, start=False, stop=False)
    return pe.matmul(out, wl, xh, start=False, stop=True)


def flat(ap):
    return ap.rearrange("p a b -> p (a b)")


class Machine:

    def __init__(self, ctx, nc, ins, out):
        self.nc, self.ins, self.out = nc, ins, out
        self.taken = []

        def sb(name, shape, dt=F32):
            return ctx.enter_context(nc.sbuf_tensor(name, shape, dt))

        self.x = sb("x", [P, NT, P])
        self.xn = sb("xn", [P, NT, P])
        self.xn2 = sb("xn2", [P, NT, P])
        self.xt = sb("xt", [P, T])
        self.mats = sb("mats", [P, len(MATS), P])
        self.cols = sb("cols", [P, len(COLS)])
        self.rows = sb("rows", [1, sum(w for _, w in ROWS)])
        self.mask = sb("mask", [P, 2, NMASK])
        self.mask2 = sb("mask2", [P, 2])
        self.w2 = sb("w2", [P, 1024])
        self.stats = sb("stats", [P, NT, 6])
        self.mv = sb("mv", [P, NT, 2])
        self.var = sb("var", [P, NT])
        self.rstd = sb("rstd", [P, NT])
        self.mhalf = sb("mhalf", [P, NT])
        self.small = sb("small", [P, 64])
        self.gates = [sb(f"gate{i}", [P, NT * 8]) for i in range(4)]
        self.arena = sb("arena", [P, 32300])
        self.parts = sb("parts", [P, 6144], F32R)
        self.bank = [ctx.enter_context(nc.psum_tensor(f"bank{i}", [P, 512], F32)) for i in range(8)]
        self.loaded = self.sem("consts_loaded")
        self.x_loaded = self.sem("x_loaded")
        self.ln_var = self.sem("ln_var")
        self.ln_rstd = self.sem("ln_rstd")
        self.ln_norm = self.sem("ln_norm")
        self.ln_turned = self.sem("ln_turned")
        self.ln_out = self.sem("ln_out")
        self.ready = self.sem("mhalf_ready")
        self.cleared = self.sem("cleared")
        self.n_ln = 0
        self.n_turn = 0

    def sem(self, name):
        self.taken.append(self.nc.alloc_semaphore(name=name))
        return self.taken[-1]

    def sems(self, prefix, names):
        return namedtuple("Sems", names)(*[self.sem(f"{prefix}_{n}") for n in names.split()])

    def carve(self, *shapes, of=None):
        at, out = 0, []
        for shape in shapes:
            n = int(np.prod(shape))
            v = (of or self.arena)[:, at:at + n]
            if len(shape) == 2:
                v = v.rearrange("p (a b) -> p a b", a=shape[0])
            elif len(shape) == 3:
                v = v.rearrange("p (a b c) -> p a b c", a=shape[0], b=shape[1])
            out.append(v)
            at += n
        assert at <= (6144 if of else 32300), at
        return out

    def mat(self, name):
        return self.mats[:, MATS.index(name), :]

    def col(self, name):
        i = COLS.index(name)
        return self.cols[:, i:i + 1]

    def row(self, name, at=0, width=None):
        start = 0
        for n, w in ROWS:
            if n == name:
                return self.rows[0:1, start + at:start + at + (width or w)]
            start += w
        raise KeyError(name)

    def row_at(self, name, at, width):
        start = 0
        for n, w in ROWS:
            if n == name:
                return self.rows[0:1, ds(at + start, width)]
            start += w
        raise KeyError(name)


class Norm:

    def __init__(self, m, src, dst):
        self.m, self.src, self.dst = m, src, dst
        self.n = m.n_ln
        m.n_ln += 1

    def dve(self, eng, ch):
        m = self.m

        def stats(b):
            t0, t1 = TB * b, TB * b + TB
            for t in range(t0, t1):
                last = eng.bn_stats(m.stats[:, t, :], self.src[:, t, :])
            ch.link(last)
            for t in range(t0, t1):
                last = eng.bn_aggr(m.mv[:, t, :], m.stats[:, t, :])
            ch.link(last)
            eng.tensor_scalar(m.var[:, t0:t1], m.mv[:, t0:t1, 1], LN_EPS, None, ALU.add).then_inc(m.ln_var, 1)

        def norm(b):
            eng.wait_ge(m.ln_rstd, B * self.n + b + 1)
            for t in range(TB * b, TB * b + TB):
                last = eng.tensor_scalar(self.dst[:, t, :], self.src[:, t, :], m.mv[:, t, 0:1],
                                         m.rstd[:, t:t + 1], ALU.subtract, ALU.mult)
            last.then_inc(m.ln_norm, 1)

        stats(0)
        for b in range(1, B):
            stats(b)
            norm(b - 1)
        norm(B - 1)
        eng.wait_ge(m.ln_norm, B * self.n + B)

    def pool(self, eng):
        m = self.m
        for b in range(B):
            eng.wait_ge(m.ln_var, B * self.n + b + 1)
            sl = slice(TB * b, TB * b + TB)
            eng.tensor_tensor(m.rstd[:, sl], m.var[:, sl], m.mhalf[:, sl], ALU.pow).then_inc(m.ln_rstd, 1)


class Turn:

    def __init__(self, m, norm, outs):
        self.m, self.norm, self.outs = m, norm, outs
        self.n = m.n_turn
        m.n_turn += 1

    def pe(self, eng):
        m = self.m
        for b in range(B):
            eng.wait_ge(m.ln_norm, B * self.norm.n + b + 1)
            k = B * self.n + b
            if k >= 2:
                eng.wait_ge(m.ln_out, k - 1)
            for q in range(TB):
                last = eng.transpose(m.bank[6 + b % 2][:, q * P:q * P + P], self.norm.dst[:, TB * b + q, :],
                                     m.mat("ident"))
            last.then_inc(m.ln_turned, 1)

    def act(self, eng):
        m = self.m
        for b in range(B):
            eng.wait_ge(m.ln_turned, B * self.n + b + 1)
            for out, gain, bias in self.outs:
                dst = out(b)
                src = m.bank[6 + b % 2][:, :]
                if gain is None:
                    last = eng.activation(dst, src, ACT.Copy)
                else:
                    last = eng.activation(dst, src, ACT.Identity, bias=m.col(bias), scale=m.col(gain))
            last.then_inc(m.ln_out, 1)

    def wait(self, eng, b=B - 1):
        eng.wait_ge(self.m.ln_out, B * self.n + b + 1)


class Consts:

    def __init__(self, m):
        self.m = m

    def sync(self, eng):
        m = self.m
        xv = m.ins["x"].rearrange("b (t p) d -> p (b t) d", p=P)
        for b in range(B):
            eng.dma_start(m.x[:, TB * b:TB * b + TB, :], xv[:, TB * b:TB * b + TB, :]).then_inc(m.x_loaded, 16)
        for name, dst in [("mats", m.mats), ("cols", m.cols), ("rows", m.rows), ("mask", m.mask),
                          ("mask2", m.mask2), ("w2", m.w2)]:
            eng.dma_start(dst[:, :] if len(dst.shape) == 2 else dst[:, :, :],
                          m.ins[name]).then_inc(m.loaded, 16)

    def wait(self, eng):
        eng.wait_ge(self.m.loaded, CONSTS)

    def pool(self, eng):
        eng.memset(self.m.mhalf[:, :], -0.5).then_inc(self.m.ready, 1)
        eng.wait_ge(self.m.ready, 1)


class MixFfn:

    def __init__(self, m, call):
        self.m = m
        self.s = m.sems(f"l0f{call}",
            "mixed k_ready rz_ready relu tanh act v_ready done")
        self.pad, self.mix, self.tmp, self.relu, self.act_k, self.th, self.a = m.carve(
            (B, S + 1), (2, T), (2, T), (T,), (T,), (T,), (2, S))
        self.norm = Norm(m, m.x, m.xn)
        self.turn = Turn(m, self.norm, [(lambda b: self.pad[:, b, 1:S + 1], None, None)])

    def sync(self, eng):
        pass

    def pool(self, eng):
        self.norm.pool(eng)

    def dve(self, eng, ch):
        m, s = self.m, self.s
        self.norm.dve(eng, ch)
        eng.wait_ge(m.loaded, CONSTS)
        eng.memset(self.pad[:, :, 0:1], 0.0)
        last = eng.tensor_scalar(m.small[:, 0:1], m.col("mu_r"), -1.0, 1.0, ALU.mult, ALU.add)
        last = eng.tensor_scalar(m.small[:, 1:2], m.col("mu_k"), -1.0, 1.0, ALU.mult, ALU.add)
        ch.link(last)
        for b in range(B):
            self.turn.wait(eng, b)
            cur, prev = self.pad[:, b, 1:S + 1], self.pad[:, b, 0:S]
            for i in range(2):
                last = eng.tensor_scalar(self.tmp[:, i, b * S:b * S + S], prev, m.small[:, i:i + 1], None, ALU.mult)
            ch.link(last)
            for i, mu in enumerate(("mu_r", "mu_k")):
                last = eng.scalar_tensor_tensor(out=self.mix[:, i, b * S:b * S + S], in0=cur, scalar=m.col(mu),
                                                in1=self.tmp[:, i, b * S:b * S + S], op0=ALU.mult, op1=ALU.add)
            last.then_inc(s.mixed, 1)
        for b in range(B):
            eng.wait_ge(s.relu, b + 1)
            sl = slice(b * S, b * S + S)
            eng.tensor_tensor(self.act_k[:, sl], self.relu[:, sl], self.relu[:, sl], ALU.mult).then_inc(s.act, 1)
        for b in range(B):
            eng.wait_ge(s.tanh, b + 1)
            eng.wait_ge(s.v_ready, b + 1)
            ch.link(eng.scalar_tensor_tensor(out=self.a[:, b % 2, :], in0=self.th[:, b * S:b * S + S], scalar=1.0,
                                             in1=m.bank[4 + b % 2][:, :], op0=ALU.add, op1=ALU.mult))
            xs = flat(m.x[:, TB * b:TB * b + TB, :])
            last = eng.scalar_tensor_tensor(out=xs, in0=self.a[:, b % 2, :], scalar=0.25, in1=xs,
                                            op0=ALU.mult, op1=ALU.add)
            last.then_inc(s.done, 1)
        eng.wait_ge(s.done, B)

    def pe(self, eng):
        m, s = self.m, self.s
        self.turn.pe(eng)
        for b in range(B):
            eng.wait_ge(s.mixed, b + 1)
            if b >= 2:
                eng.wait_ge(s.relu, b - 1)
                eng.wait_ge(s.tanh, b - 1)
            eng.matmul(m.bank[b % 2][:, :], m.mat("Wk"), self.mix[:, 1, b * S:b * S + S], start=True,
                       stop=True).then_inc(s.k_ready, 1)
            for q in range(TB):
                t = b * S + q * P
                last = eng.matmul(m.bank[2 + b % 2][:, q * P:q * P + P], self.mix[:, 0, t:t + P], m.mat("Wr"),
                                  start=True, stop=True)
            last.then_inc(s.rz_ready, 1)
        for b in range(B):
            eng.wait_ge(s.act, b + 1)
            if b >= 2:
                eng.wait_ge(s.done, b - 1)
            for q in range(TB):
                t = b * S + q * P
                last = eng.matmul(m.bank[4 + b % 2][:, q * P:q * P + P], self.act_k[:, t:t + P], m.mat("Wv"),
                                  start=True, stop=True)
            last.then_inc(s.v_ready, 1)

    def act(self, eng):
        m, s = self.m, self.s
        self.turn.act(eng)
        for b in range(B):
            eng.wait_ge(s.k_ready, b + 1)
            eng.activation(self.relu[:, b * S:b * S + S], m.bank[b % 2][:, :], ACT.Relu).then_inc(s.relu, 1)
            eng.wait_ge(s.rz_ready, b + 1)
            eng.activation(self.th[:, b * S:b * S + S], m.bank[2 + b % 2][:, :], ACT.Tanh,
                           scale=0.5).then_inc(s.tanh, 1)


def rank_of(eng, ch, v, n, greater, equal, tri, rank):
    g = greater.rearrange("p (t a b) -> p t a b", t=NT, a=n)
    q = equal.rearrange("p (t a b) -> p t a b", t=NT, a=n)
    other = v.unsqueeze(2).to_broadcast([P, NT, n, n])
    own = v.unsqueeze(3).to_broadcast([P, NT, n, n])
    eng.tensor_tensor(g, other, own, ALU.is_gt)
    ch.link(eng.tensor_tensor(q, other, own, ALU.is_equal))
    ch.link(eng.tensor_tensor(q, q, tri.unsqueeze(1).to_broadcast([P, NT, n, n]), ALU.mult))
    ch.link(eng.tensor_tensor(greater, greater, equal, ALU.add))
    ch.link(eng.tensor_reduce(rank, g, AX.X, ALU.add))


class GeluMoe:

    RING = HID + 2 * HID + 2 * P + 4

    def __init__(self, m, call):
        self.m = m
        self.s = m.sems(f"l1f{call}", "const logits exp_in exp w_ready turned wt bias_ready h1_ready h2_ready "
                                      "gelu1 gelu2 y_ready added load0 load1 x_split w_split")
        ring0, ring1, self.h1, self.h2, self.gw, self.gb, self.b3, self.tri, self.w, self.g, self.q, \
            self.wt, self.tmp = m.carve((self.RING,), (self.RING,), (2, S), (2, S), (NE,), (NT, NE), (P,),
                              (NE, NE), (NT, NE), (NT * 64,), (NT * 64,), (T,), (T,))
        self.xh, self.xl, wh, wl = m.carve((T,), (T,), (2, HID), (2, HID), of=m.parts)
        self.wh, self.wl = [wh[:, k, :] for k in range(2)], [wl[:, k, :] for k in range(2)]
        self.ring = [ring0, ring1]
        self.norm = Norm(m, m.x, m.xn)
        self.turn = Turn(m, self.norm, [(lambda b: m.xt[:, b * S:b * S + S], None, None)])

    def sync(self, eng):
        m, s = self.m, self.s
        eng.wait_ge(m.ln_var, B * self.norm.n + 1)
        eng.dma_start(self.gw, m.ins["l1_gate_w"]).then_inc(s.const, 16)
        eng.dma_start(self.gb, m.ins["l1_gate_b"]).then_inc(s.const, 16)
        eng.dma_start(self.b3[0:NE, :], m.ins["l1_b3"]).then_inc(s.const, 16)
        eng.dma_start(self.tri, m.ins["tri8"]).then_inc(s.const, 16)
        for k in range(2):
            eng.dma_start(self.ring[k], m.ins["l1_w"][k]).then_inc([s.load0, s.load1][k], 16)
        with eng.Fori(1, NE // 2) as i:
            for k in range(2):
                eng.wait_ge(s.y_ready, (i * 2 + (k - 1)) * B)
                eng.dma_start(self.ring[k], m.ins["l1_w"][ds(i * 2 + k, 1)].rearrange("e p n -> p (e n)")
                              ).then_inc([s.load0, s.load1][k], 16)

    def pool(self, eng):
        self.norm.pool(eng)

    def dve(self, eng, ch):
        m, s = self.m, self.s
        self.norm.dve(eng, ch)
        self.turn.wait(eng)
        split(eng, ch.link, m.xt[:, :], self.tmp, self.xh, self.xl).then_inc(s.x_split, 1)
        eng.wait_ge(s.x_split, 1)
        eng.wait_ge(s.load0, 16)
        self.split_weights(eng, 0, 1)
        eng.wait_ge(s.const, 64)
        eng.wait_ge(s.logits, 1)
        z, zx = m.gates[0], m.gates[1]
        z3 = z[:, :].rearrange("p (t e) -> p t e", e=NE)
        ch.link(eng.tensor_tensor(z3, m.bank[5][:, 0:NT * NE].rearrange("p (t e) -> p t e", e=NE), self.gb, ALU.add))
        softmax_in(eng, ch, m, z3, s.exp_in)
        eng.wait_ge(s.exp, 1)
        p3 = softmax_out(eng, ch, m, z3)
        rank = m.gates[3][:, :].rearrange("p (t e) -> p t e", e=NE)
        rank_of(eng, ch, p3, NE, self.g, self.q, self.tri, rank)
        ch.link(eng.tensor_scalar(rank, rank, 1.5, 0.5, ALU.is_lt, ALU.mult))
        ch.link(eng.tensor_tensor(self.w, rank, p3, ALU.mult))
        eng.sem_inc(s.w_ready, 1)
        for b in range(B):
            eng.wait_ge(s.turned, b + 1)
            eng.tensor_copy(self.wt[0:NE, b * S:b * S + S], m.bank[b][0:NE, :]).then_inc(s.wt, 1)
        for b in range(B):
            eng.wait_ge(s.bias_ready, b + 1)
            xs = flat(m.x[:, TB * b:TB * b + TB, :])
            last = eng.tensor_tensor(xs, m.bank[4 + b % 2][:, :], xs, ALU.add)
            last.then_inc(s.added, PRIME // 4)
        def experts(i, last_pair):
            for k in range(2):
                for b in range(B):
                    n = (i * 2 + k) * B + b
                    eng.wait_ge(s.y_ready, n + 1)
                    eng.wait_ge(s.added, n + PRIME)
                    for q in range(TB):
                        t = TB * b + q
                        last = eng.scalar_tensor_tensor(
                            out=m.x[:, t, :], in0=m.bank[4 + b % 2][:, q * P:q * P + P],
                            scalar=self.w[:, t, ds(i * 2 + k, 1)], in1=m.x[:, t, :], op0=ALU.mult, op1=ALU.add)
                    last.then_inc(s.added, 1)
                    if b == 1 and not (last_pair and k == 1):
                        eng.wait_ge([s.load1, s.load0][k], (i + k) * 16 + 16)
                        self.split_weights(eng, 1 - k, i * 2 + (k + 2))

        with eng.Fori(0, NE // 2 - 1) as i:
            experts(i, False)
        experts(NE // 2 - 1, True)
        eng.wait_ge(s.added, NE * B + PRIME)

    def split_weights(self, eng, k, n):
        s = self.s

        def link(ins):
            ins.then_inc(s.w_split, 1)
            eng.wait_ge(s.w_split, n * 2 - 1)

        if not (isinstance(n, int) and n == 1):
            eng.wait_ge(s.w_split, n * 2 - 2)
        split(eng, link, self.ring[k][:, 0:HID], self.tmp[:, 0:HID], self.wh[k], self.wl[k]).then_inc(s.w_split, 1)

    def pe(self, eng):
        m, s = self.m, self.s
        self.turn.pe(eng)
        eng.wait_ge(s.const, 64)
        self.turn.wait(eng)
        for t in range(NT):
            last = eng.matmul(m.bank[5][:, t * NE:t * NE + NE], m.xt[:, t * P:t * P + P], self.gw,
                              start=True, stop=True)
        last.then_inc(s.logits, 1)

        def ring(k):
            r = self.ring[k]
            return (r[:, HID:3 * HID].rearrange("p (a n) -> p a n", a=2),
                    r[:, 3 * HID:3 * HID + 2 * P].rearrange("p (a n) -> p a n", a=2))

        def first(k, b):
            for j in range(2):
                product(eng, m.bank[j][:, :], (self.wh[k][:, j * P:j * P + P], self.wl[k][:, j * P:j * P + P]),
                        (self.xh[:, b * S:b * S + S], self.xl[:, b * S:b * S + S])).then_inc(s.h1_ready, 1)

        def second(n, k, b):
            eng.wait_ge(s.gelu1, 2 * n + 2)
            for j in range(2):
                for a in range(2):
                    last = eng.matmul(m.bank[2 + j][:, :], ring(k)[0][:, a, j * P:j * P + P], self.h1[:, a, :],
                                      start=(a == 0), stop=(a == 1))
                last.then_inc(s.h2_ready, 1)

        def third(n, k, b):
            eng.wait_ge(s.gelu2, 2 * n + 2)
            eng.wait_ge(s.added, n - 1 + PRIME)
            for q in range(TB):
                for a in range(2):
                    last = eng.matmul(m.bank[4 + b % 2][:, q * P:q * P + P], self.h2[:, a, q * P:q * P + P],
                                      ring(k)[1][:, a, :], start=(a == 0), stop=(a == 1))
            last.then_inc(s.y_ready, 1)

        eng.wait_ge(s.w_ready, 1)
        for b in range(B):
            for q in range(TB):
                last = eng.transpose(m.bank[b][0:NE, q * P:q * P + P], self.w[:, TB * b + q, :], m.mat("ident"))
            last.then_inc(s.turned, 1)
        for b in range(B):
            eng.wait_ge(s.wt, b + 1)
            if b >= 2:
                eng.wait_ge(s.added, (b - 1) * PRIME // 4)
            for q in range(TB):
                t = b * S + q * P
                last = eng.matmul(m.bank[4 + b % 2][:, q * P:q * P + P], self.wt[0:NE, t:t + P], self.b3[0:NE, :],
                                  start=True, stop=True)
            last.then_inc(s.bias_ready, 1)
        eng.wait_ge(s.x_split, 1)
        eng.wait_ge(s.w_split, 2)
        first(0, 0)

        def experts(i, last_pair):
            for k in range(2):
                for b in range(B):
                    n = (i * 2 + k) * B + b
                    second(n, k, b)
                    if b + 1 < B:
                        first(k, b + 1)
                    elif k == 0:
                        eng.wait_ge(s.w_split, i * 4 + 4)
                        first(1, 0)
                    elif not last_pair:
                        eng.wait_ge(s.w_split, i * 4 + 6)
                        first(0, 0)
                    third(n, k, b)

        with eng.Fori(0, NE // 2 - 1) as i:
            experts(i, False)
        experts(NE // 2 - 1, True)

    def act(self, eng):
        m, s = self.m, self.s
        self.turn.act(eng)
        eng.wait_ge(s.exp_in, 1)
        eng.activation(m.gates[1][:, :], m.gates[0][:, :], ACT.Exp).then_inc(s.exp, 1)
        eng.wait_ge(s.load0, 16)

        def gelus(n, k, which):
            ready, done, h, at = [(s.h1_ready, s.gelu1, self.h1, 0), (s.h2_ready, s.gelu2, self.h2, 2)][which]
            for j in range(2):
                eng.wait_ge(ready, 2 * n + j + 1)
                c = self.RING - 4 + at + j
                eng.activation(h[:, j, :], m.bank[2 * which + j][:, :], ACT.Gelu,
                               bias=self.ring[k][:, c:c + 1]).then_inc(done, 1)

        gelus(0, 0, 0)

        def experts(i, last_pair):
            for k in range(2):
                for b in range(B):
                    n = (i * 2 + k) * B + b
                    gelus(n, k, 1)
                    if b + 1 < B:
                        gelus(n + 1, k, 0)
                    elif k == 0:
                        eng.wait_ge(s.load1, i * 16 + 16)
                        gelus(n + 1, 1, 0)
                    elif not last_pair:
                        eng.wait_ge(s.load0, i * 16 + 32)
                        gelus(n + 1, 0, 0)

        with eng.Fori(0, NE // 2 - 1) as i:
            experts(i, False)
        experts(NE // 2 - 1, True)


def softmax_in(eng, ch, m, z3, ready):
    mx = m.small[:, 16:16 + NT]
    ch.link(eng.tensor_reduce(mx, z3, AX.X, ALU.max))
    eng.tensor_tensor(z3, z3, mx.unsqueeze(2).to_broadcast([P, NT, NE]), ALU.subtract).then_inc(ready, 1)


def softmax_out(eng, ch, m, z3):
    sm, rc = m.small[:, 16:16 + NT], m.small[:, 32:32 + NT]
    e3 = m.gates[1][:, :].rearrange("p (t e) -> p t e", e=NE)
    p3 = m.gates[2][:, :].rearrange("p (t e) -> p t e", e=NE)
    ch.link(eng.tensor_reduce(sm, e3, AX.X, ALU.add))
    ch.link(eng.reciprocal(rc, sm))
    ch.link(eng.tensor_tensor(p3, e3, rc.unsqueeze(2).to_broadcast([P, NT, NE]), ALU.mult))
    return p3


class SwigluMoe:

    def __init__(self, m, call):
        self.m = m
        self.s = m.sems(f"l3f{call}",
            "const logits exp_in exp up_ready g_ready silu h_ready y_ready "
            "added load0 load1 x_split w_split")
        ring0, ring1, self.sg, self.h, self.gw, self.tri, self.w, self.g, self.q, self.xa, self.tmp = m.carve(
            (3 * HID,), (3 * HID,), (2, S), (2, 2, S), (NE,), (NE, NE), (NT, NE + 1), (NT * 64,), (NT * 64,),
            (T,), (T,))
        self.xh, self.xl, wh, wl = m.carve((T,), (T,), (2, 2 * HID), (2, 2 * HID), of=m.parts)
        self.wh, self.wl = [wh[:, k, :] for k in range(2)], [wl[:, k, :] for k in range(2)]
        self.ring = [ring0, ring1]
        self.norm = Norm(m, m.x, m.xn)
        self.turn = Turn(m, self.norm, [(lambda b: m.xt[:, b * S:b * S + S], None, None)])
        self.norm2 = Norm(m, m.xn, m.xn2)
        self.turn2 = Turn(m, self.norm2, [(lambda b: self.xa[:, b * S:b * S + S], "l3_s", "l3_b")])

    def sync(self, eng):
        m, s = self.m, self.s
        eng.wait_ge(m.ln_var, B * self.norm.n + 1)
        eng.dma_start(self.gw, m.ins["l3_gate_w"]).then_inc(s.const, 16)
        eng.dma_start(self.tri, m.ins["tri8"]).then_inc(s.const, 16)
        for k in range(2):
            eng.dma_start(self.ring[k], m.ins["l3_w"][k]).then_inc([s.load0, s.load1][k], 16)

        def load(e, k):
            eng.wait_ge(s.y_ready, (e - 1) * B)
            eng.dma_start(self.ring[k], m.ins["l3_w"][ds(e, 1)].rearrange("e p n -> p (e n)")
                          ).then_inc([s.load0, s.load1][k], 16)

        with eng.Fori(1, NE // 2) as i:
            load(i * 2, 0)
            load(i * 2 + 1, 1)
        eng.wait_ge(s.y_ready, (NE - 1) * B)
        eng.dma_start(self.ring[0], m.ins["l3_w"][NE]).then_inc(s.load0, 16)

    def pool(self, eng):
        self.norm.pool(eng)
        self.norm2.pool(eng)

    def dve(self, eng, ch):
        m, s = self.m, self.s
        self.norm.dve(eng, ch)
        self.norm2.dve(eng, ch)
        self.turn.wait(eng)
        split(eng, ch.link, m.xt[:, :], self.tmp, self.xh, self.xl).then_inc(s.x_split, 1)
        eng.wait_ge(s.x_split, 1)
        eng.wait_ge(s.load0, 16)
        self.split_weights(eng, 0, 1)
        eng.wait_ge(s.const, 32)
        eng.wait_ge(s.logits, 1)
        z3 = m.gates[0][:, :].rearrange("p (t e) -> p t e", e=NE)
        ch.link(eng.tensor_copy(m.gates[0][:, :], m.bank[4][:, 0:NT * NE]))
        softmax_in(eng, ch, m, z3, s.exp_in)
        eng.wait_ge(s.exp, 1)
        p3 = softmax_out(eng, ch, m, z3)
        rank = m.gates[3][:, :].rearrange("p (t e) -> p t e", e=NE)
        rank_of(eng, ch, p3, NE, self.g, self.q, self.tri, rank)
        sm, rc = m.small[:, 16:16 + NT], m.small[:, 32:32 + NT]
        ch.link(eng.tensor_scalar(rank, rank, 1.5, None, ALU.is_lt))
        ch.link(eng.tensor_tensor(rank, rank, p3, ALU.mult))
        ch.link(eng.tensor_reduce(sm, rank, AX.X, ALU.add))
        ch.link(eng.tensor_scalar(sm, sm, 1e-5, 2.0, ALU.add, ALU.mult))
        ch.link(eng.reciprocal(rc, sm))
        ch.link(eng.tensor_tensor(self.w[:, :, 1:NE + 1], rank, rc.unsqueeze(2).to_broadcast([P, NT, NE]), ALU.mult))
        ch.link(eng.memset(self.w[:, :, 0:1], 0.5))
        eng.sem_inc(s.added, PRIME)

        def hidden(n, b):
            eng.wait_ge(s.up_ready, n + 1)
            for j in range(2):
                eng.wait_ge(s.silu, 2 * n + j + 1)
                eng.tensor_tensor(self.h[:, b % 2, j, :], self.sg[:, j, :], m.bank[2 + j][:, :],
                                  ALU.mult).then_inc(s.h_ready, 1)

        def add(n, e, b):
            eng.wait_ge(s.y_ready, n + 1)
            eng.wait_ge(s.added, n + PRIME)
            for q in range(TB):
                t = TB * b + q
                last = eng.scalar_tensor_tensor(
                    out=m.x[:, t, :], in0=m.bank[4 + b % 2][:, q * P:q * P + P],
                    scalar=self.w[:, t, ds(e, 1)], in1=m.x[:, t, :], op0=ALU.mult, op1=ALU.add)
            last.then_inc(s.added, 1)

        hidden(0, 0)
        with eng.Fori(0, NE // 2) as i:
            for k in range(2):
                for b in range(B):
                    e = i * 2 + k
                    n = e * B + b
                    hidden(n + 1, (b + 1) % B)
                    add(n, e, b)
                    if b == 1:
                        eng.wait_ge([s.load1, s.load0][k], (i + k) * 16 + 16)
                        self.split_weights(eng, 1 - k, e + 2)
        for b in range(B):
            if b + 1 < B:
                hidden(NE * B + b + 1, b + 1)
            add(NE * B + b, NE, b)
        eng.wait_ge(s.added, (NE + 1) * B + PRIME)

    def split_weights(self, eng, k, n):
        s = self.s

        def link(ins):
            ins.then_inc(s.w_split, 1)
            eng.wait_ge(s.w_split, n * 2 - 1)

        if not (isinstance(n, int) and n == 1):
            eng.wait_ge(s.w_split, n * 2 - 2)
        split(eng, link, self.ring[k][:, 0:2 * HID], self.tmp[:, 0:2 * HID], self.wh[k], self.wl[k]).then_inc(s.w_split, 1)

    def pe(self, eng):
        m, s = self.m, self.s
        self.turn.pe(eng)
        self.turn2.pe(eng)
        eng.wait_ge(s.const, 32)
        self.turn2.wait(eng)
        for t in range(NT):
            last = eng.matmul(m.bank[4][:, t * NE:t * NE + NE], self.xa[:, t * P:t * P + P], self.gw,
                              start=True, stop=True)
        last.then_inc(s.logits, 1)

        def up(n, k, b):
            if n is not None:
                eng.wait_ge(s.h_ready, 2 * n)
            for half, first in ((0, 0), (1, 2)):
                for j in range(2):
                    at = half * HID + j * P
                    last = product(eng, m.bank[first + j][:, :], (self.wh[k][:, at:at + P], self.wl[k][:, at:at + P]),
                                   (self.xh[:, b * S:b * S + S], self.xl[:, b * S:b * S + S]))
                    if half == 0:
                        last.then_inc(s.g_ready, 1)
            last.then_inc(s.up_ready, 1)

        def down(n, k, b):
            eng.wait_ge(s.h_ready, 2 * n + 2)
            eng.wait_ge(s.added, n - 1 + PRIME)
            w = self.ring[k][:, 2 * HID:3 * HID].rearrange("p (a n) -> p a n", a=2)
            for q in range(TB):
                for a in range(2):
                    last = eng.matmul(m.bank[4 + b % 2][:, q * P:q * P + P], self.h[:, b % 2, a, q * P:q * P + P],
                                      w[:, a, :], start=(a == 0), stop=(a == 1))
            last.then_inc(s.y_ready, 1)

        eng.wait_ge(s.x_split, 1)
        eng.wait_ge(s.w_split, 2)
        up(None, 0, 0)
        with eng.Fori(0, NE // 2) as i:
            for k in range(2):
                for b in range(B):
                    n = (i * 2 + k) * B + b
                    if b == B - 1:
                        eng.wait_ge(s.w_split, (i * 2 + (k + 2)) * 2)
                    up(n + 1, k if b < B - 1 else 1 - k, (b + 1) % B)
                    down(n, k, b)
        for b in range(B):
            n = NE * B + b
            if b + 1 < B:
                up(n + 1, 0, b + 1)
            down(n, 0, b)

    def act(self, eng):
        m, s = self.m, self.s
        self.turn.act(eng)
        self.turn2.act(eng)
        eng.wait_ge(s.exp_in, 1)
        eng.activation(m.gates[1][:, :], m.gates[0][:, :], ACT.Exp).then_inc(s.exp, 1)

        def silus(n):
            for j in range(2):
                eng.wait_ge(s.g_ready, 2 * n + j + 1)
                eng.activation(self.sg[:, j, :], m.bank[j][:, :], ACT.Silu).then_inc(s.silu, 1)

        with eng.Fori(0, (NE + 1) // 3) as i:
            for b in range(3 * B):
                silus(i * (3 * B) + b)


class RoutedMoe:

    def __init__(self, m, call):
        self.m = m
        self.s = m.sems(f"l2f{call}",
            "const logits exp turned w_ready split g_ready u_ready "
            "gate_ready silu prod hid y_done y_out y_turned added load0 "
            "load1 sel x_split w_split high middle low")
        ring0, ring1, self.sg, self.a, self.h, self.rw, self.eb, self.tri, self.sc, self.sb_, self.g, self.q, \
            self.w, self.rest, hm, lo, selh, sell, self.yt, zero, self.wcopy, self.tmp = m.carve(
                (3 * P,), (3 * P,), (2, S), (2, S), (2, S), (E2,), (NT, E2), (G2, G2), (NT, E2), (NT, E2),
                (NT * 64,), (NT * 64,), (NT, E2), (T,), (T // 2,), (T // 2,), (PAIRS * P // 2,),
                (PAIRS * P // 2,), (T,), (P // 2,), (T // 2,), (T,))
        self.xh, self.xl, wh, wl = m.carve((T,), (T,), (2, 2 * P), (2, 2 * P), of=m.parts)
        self.wh, self.wl = [wh[:, k, :] for k in range(2)], [wl[:, k, :] for k in range(2)]
        self.ring = [ring0, ring1]
        self.hm, self.lo, self.zero = hm.bitcast(BF16), lo.bitcast(BF16), zero.bitcast(BF16)
        self.wcopy = self.wcopy.bitcast(BF16)
        self.selh, self.sell = selh.bitcast(BF16), sell.bitcast(BF16)
        self.norm = Norm(m, m.x, m.xn)
        self.turn = Turn(m, self.norm, [(lambda b: m.xt[:, b * S:b * S + S], None, None)])

    def sync(self, eng):
        m, s = self.m, self.s
        eng.wait_ge(m.ln_var, B * self.norm.n + 1)
        eng.dma_start(self.rw, m.ins["l2_router"]).then_inc(s.const, 16)
        eng.dma_start(self.eb, m.ins["l2_e_bias"]).then_inc(s.const, 16)
        eng.dma_start(self.tri, m.ins["tri8"]).then_inc(s.const, 16)
        for k in range(2):
            eng.dma_start(self.ring[k], m.ins["l2_w"][k]).then_inc([s.load0, s.load1][k], 16)
        with eng.Fori(1, PAIRS // 2) as i:
            for k in range(2):
                eng.wait_ge(s.y_done, (i * 2 + (k - 1)) * B)
                eng.dma_start(self.ring[k], m.ins["l2_w"][ds(i * 2 + k, 1)].rearrange("e p n -> p (e n)")
                              ).then_inc([s.load0, s.load1][k], 16)

    def pool(self, eng):
        m, s = self.m, self.s
        self.norm.pool(eng)
        eng.wait_ge(m.ln_var, B * self.norm.n + 1)
        eng.memset(self.zero, 0.0)
        eng.memset(self.lo, 0.0)
        eng.memset(self.selh, 0.0)
        eng.memset(self.sell, 0.0).then_inc(s.sel, 1)
        eng.wait_ge(s.sel, 1)
        for n, (t, parts, base) in enumerate([(self.selh, P, 0), (self.selh, P, -E2), (self.sell, E2, 0)]):
            v = t[0:parts, 2 * P:].rearrange("p (c h u) -> p c h u", h=2, u=H2)
            eng.affine_select(out=v, in_=v, compare_op=ALU.not_equal, fill=1.0, base=base,
                              pattern=[[-2, PAIRS - 2], [-1, 2], [0, H2]], channel_multiplier=1).then_inc(s.sel, 1)
            eng.wait_ge(s.sel, n + 2)
        eng.memset(self.lo[E2:E2 + 1, :], 1.0)
        eng.memset(self.sell[E2:E2 + 1, 0:2 * P], 1.0).then_inc(s.sel, 1)

    def dve(self, eng, ch):
        m, s = self.m, self.s
        self.norm.dve(eng, ch)
        self.turn.wait(eng)
        split(eng, ch.link, m.xt[:, :], self.tmp, self.xh, self.xl).then_inc(s.x_split, 1)
        eng.wait_ge(s.x_split, 1)
        eng.wait_ge(s.load0, 16)
        self.split_weights(eng, 0, 1)
        eng.wait_ge(s.const, 48)
        sc, sb, w = self.sc, self.sb_, self.w
        for half in range(2):
            eng.wait_ge(s.exp, half + 1)
        ch.link(eng.tensor_scalar(flat(sb), flat(sc), 1.0, None, ALU.add))
        ch.link(eng.reciprocal(flat(sc), flat(sb)))
        ch.link(eng.tensor_tensor(sb, sc, self.eb, ALU.add))
        NG = NT * G2
        sb3 = sb.rearrange("p t (g e) -> p (t g) e", g=G2)
        q3 = self.q.rearrange("p (a e) -> p a e", e=8)
        g3 = self.g.rearrange("p (a e) -> p a e", e=8)
        m1, m2, cnt, gr = (m.gates[i][:, :] for i in range(4))

        def spread(v):
            return v.unsqueeze(2).to_broadcast([P, NG, 8])

        ch.link(eng.tensor_reduce(m1, sb3, AX.X, ALU.max))
        ch.link(eng.tensor_tensor(q3, sb3, spread(m1), ALU.is_equal))
        ch.link(eng.tensor_reduce(cnt, q3, AX.X, ALU.add))
        ch.link(eng.scalar_tensor_tensor(out=self.g, in0=self.q, scalar=-BIG, in1=flat(sb), op0=ALU.mult, op1=ALU.add))
        ch.link(eng.tensor_reduce(m2, g3, AX.X, ALU.max))
        ch.link(eng.tensor_scalar(cnt, cnt, 1.5, 2 * BIG, ALU.is_gt, ALU.mult))
        ch.link(eng.scalar_tensor_tensor(out=cnt, in0=cnt, scalar=-BIG, in1=m1, op0=ALU.add, op1=ALU.min))
        ch.link(eng.tensor_tensor(m2, m2, cnt, ALU.max))
        ch.link(eng.tensor_tensor(gr, m1, m2, ALU.add))
        gr3 = gr.rearrange("p (t g) -> p t g", g=G2)
        rank = m1.rearrange("p (t g) -> p t g", g=G2)
        rank_of(eng, ch, gr3, G2, self.g, self.q, self.tri, rank)
        ch.link(eng.tensor_scalar(m2, m1, 3.5, None, ALU.is_lt))
        ch.link(eng.tensor_tensor(g3, sb3, spread(m2), ALU.mult))
        ch.link(eng.tensor_scalar(m2, m2, -1.0, BIG, ALU.add, ALU.mult))
        ch.link(eng.tensor_tensor(g3, g3, spread(m2), ALU.add))
        masked = self.g.rearrange("p (t e) -> p t e", e=E2)
        left = self.q.rearrange("p (t e) -> p t e", e=E2)
        top = m.gates[0][:, :].rearrange("p (t e) -> p t e", e=8)
        for t in range(NT):
            last = eng.max(top[:, t, :], masked[:, t, :])
        ch.link(last)
        for t in range(NT):
            last = eng.match_replace(left[:, t, :], top[:, t, :], masked[:, t, :], -2 * BIG)
        ch.link(last)
        ch.link(eng.tensor_tensor(w, left, masked, ALU.not_equal))
        ch.link(eng.tensor_tensor(w, w, sc, ALU.mult))
        sm, rc = m.small[:, 16:16 + NT], m.small[:, 32:32 + NT]
        ch.link(eng.tensor_reduce(sm, w, AX.X, ALU.add))
        ch.link(eng.tensor_scalar(sm, sm, 1e-20, None, ALU.add))
        ch.link(eng.reciprocal(rc, sm))
        ch.link(eng.tensor_tensor(w, w, rc.unsqueeze(2).to_broadcast([P, NT, E2]), ALU.mult))
        eng.sem_inc(s.w_ready, 1)
        for b in range(B):
            sl = slice(b * S, b * S + S)
            rest = self.rest[0:E2, sl]
            eng.wait_ge(s.high, b + 1)
            ch.link(eng.tensor_tensor(rest, m.bank[b][0:E2, :], self.hm[0:E2, sl], ALU.subtract))
            ch.link(eng.tensor_copy(self.wcopy[0:E2, sl], rest))
            eng.tensor_copy(self.hm[E2:P, sl], self.wcopy[0:E2, sl]).then_inc(s.middle, 1)
            eng.tensor_tensor(rest, rest, self.wcopy[0:E2, sl], ALU.subtract).then_inc(s.low, 1)

        def blocks(i, last_pair):
            for k in range(2):
                for b in range(B):
                    n = (i * 2 + k) * B + b
                    eng.wait_ge(s.silu, n + 1)
                    eng.wait_ge(s.u_ready, n + 1)
                    eng.tensor_tensor(self.a[:, b % 2, :], self.sg[:, b % 2, :], m.bank[5][:, :],
                                      ALU.mult).then_inc(s.prod, 1)
                    eng.wait_ge(s.prod, n + 1)
                    eng.wait_ge(s.gate_ready, n + 1)
                    eng.tensor_tensor(self.h[:, b % 2, :], self.a[:, b % 2, :], m.bank[6][:, :],
                                      ALU.mult).then_inc(s.hid, 1)
                    if b == 1 and not (last_pair and k == 1):
                        eng.wait_ge([s.load1, s.load0][k], (i + k) * 16 + 16)
                        self.split_weights(eng, 1 - k, i * 2 + k + 2)

        with eng.Fori(0, PAIRS // 2 - 1) as i:
            blocks(i, False)
        blocks(PAIRS // 2 - 1, True)
        for b in range(B):
            eng.wait_ge(s.y_turned, b + 1)
            xs = flat(m.x[:, TB * b:TB * b + TB, :])
            eng.scalar_tensor_tensor(out=xs, in0=m.bank[4 + b % 2][:, :], scalar=0.5, in1=xs,
                                     op0=ALU.mult, op1=ALU.add).then_inc(s.added, 1)
        eng.wait_ge(s.added, B)

    def split_weights(self, eng, k, n):
        s = self.s

        def link(ins):
            ins.then_inc(s.w_split, 1)
            eng.wait_ge(s.w_split, n * 2 - 1)

        if not (isinstance(n, int) and n == 1):
            eng.wait_ge(s.w_split, n * 2 - 2)
        split(eng, link, self.ring[k][:, 0:2 * P], self.tmp[:, 0:2 * P], self.wh[k], self.wl[k]).then_inc(s.w_split, 1)

    def pe(self, eng):
        m, s = self.m, self.s
        self.turn.pe(eng)
        eng.wait_ge(s.const, 48)
        self.turn.wait(eng)
        for t in range(NT):
            last = eng.matmul(m.bank[4 + t // 8][:, t % 8 * E2:t % 8 * E2 + E2], m.xt[:, t * P:t * P + P], self.rw,
                              start=True, stop=True)
            if t % 8 == 7:
                last.then_inc(s.logits, 1)
        eng.wait_ge(s.w_ready, 1)
        for b in range(B):
            for q in range(TB):
                last = eng.transpose(m.bank[b][0:E2, q * P:q * P + P], self.w[:, TB * b + q, :], m.mat("ident"))
            last.then_inc(s.turned, 1)

        def tokens(b):
            return self.xh[:, b * S:b * S + S], self.xl[:, b * S:b * S + S]

        def gate(k, b):
            product(eng, m.bank[4][:, :], (self.wh[k][:, 0:P], self.wl[k][:, 0:P]), tokens(b)).then_inc(s.g_ready, 1)

        def up(k, b):
            product(eng, m.bank[5][:, :], (self.wh[k][:, P:2 * P], self.wl[k][:, P:2 * P]),
                    tokens(b)).then_inc(s.u_ready, 1)

        def spread(p, b):
            sl = slice(b * S, b * S + S)
            eng.matmul(m.bank[6][:, :], self.selh[:, ds(p * P, P)], self.hm[:, sl], start=True, stop=False)
            eng.matmul(m.bank[6][:, :], self.sell[:, ds(p * P, P)], self.lo[:, sl], start=False,
                       stop=True).then_inc(s.gate_ready, 1)

        def down(k, b, stop):
            eng.matmul(m.bank[b][:, :], self.ring[k][:, 2 * P:3 * P], self.h[:, b % 2, :], start=False, stop=stop,
                       skip_group_check=True).then_inc(s.y_done, 1)

        eng.wait_ge(s.x_split, 1)
        eng.wait_ge(s.w_split, 2)
        gate(0, 0)
        up(0, 0)
        eng.wait_ge(s.split, B)
        eng.wait_ge(s.middle, B)
        eng.wait_ge(s.sel, 5)
        for b in range(B):
            eng.matmul(m.bank[b][:, :], self.zero, self.hm[:, b * S:b * S + S], start=True, stop=False,
                       skip_group_check=True)
        spread(0, 0)

        def blocks(i, last_pair):
            for k in range(2):
                for b in range(B):
                    p = i * 2 + k
                    n = p * B + b
                    end = last_pair and k == 1 and b == B - 1
                    k2 = k if b < B - 1 else 1 - k
                    b2 = (b + 1) % B
                    if not end:
                        if b == B - 1:
                            eng.wait_ge(s.w_split, (p + 2) * 2)
                        eng.wait_ge(s.silu, n + 1)
                        gate(k2, b2)
                        eng.wait_ge(s.prod, n + 1)
                        up(k2, b2)
                    eng.wait_ge(s.hid, n + 1)
                    down(k, b, last_pair and k == 1)
                    if not end:
                        spread(p if b < B - 1 else p + 1, b2)

        with eng.Fori(0, PAIRS // 2 - 1) as i:
            blocks(i, False)
        blocks(PAIRS // 2 - 1, True)
        for b in range(B):
            eng.wait_ge(s.y_out, b + 1)
            if b >= 2:
                eng.wait_ge(s.added, b - 1)
            for q in range(TB):
                t = b * S + q * P
                last = eng.transpose(m.bank[4 + b % 2][:, q * P:q * P + P], self.yt[:, t:t + P], m.mat("ident"))
            last.then_inc(s.y_turned, 1)

    def act(self, eng):
        m, s = self.m, self.s
        self.turn.act(eng)
        for half in range(2):
            eng.wait_ge(s.logits, half + 1)
            out = flat(self.sc[:, half * 8:half * 8 + 8, :])
            eng.activation(out, m.bank[4 + half][:, :], ACT.Exp, scale=-1.0).then_inc(s.exp, 1)
        eng.wait_ge(s.sel, 1)
        for b in range(B + 1):
            if b < B:
                eng.wait_ge(s.turned, b + 1)
                eng.activation(self.hm[0:E2, b * S:b * S + S], m.bank[b][0:E2, :], ACT.Copy).then_inc(s.high, 1)
            if b:
                sl = slice(b * S - S, b * S)
                eng.wait_ge(s.low, b)
                eng.activation(self.lo[0:E2, sl], self.rest[0:E2, sl], ACT.Copy).then_inc(s.split, 1)
        with eng.Fori(0, PAIRS // 2) as p:
            for b in range(2 * B):
                n = p * (2 * B) + b
                eng.wait_ge(s.g_ready, n + 1)
                eng.activation(self.sg[:, b % 2, :], m.bank[4][:, :], ACT.Silu).then_inc(s.silu, 1)
        for b in range(B):
            eng.wait_ge(s.y_done, (PAIRS - 1) * B + b + 1)
            eng.activation(self.yt[:, b * S:b * S + S], m.bank[b][:, :], ACT.Copy).then_inc(s.y_out, 1)


class Core:

    def __init__(self, m, name, units, bufs, q, keys, extra, masked, v, out, dv, wrap, turns, shared, lag, arrived=None):
        self.m, self.units, self.q, self.keys, self.extra = m, units, q, keys, extra
        self.lag = lag
        self.turns, self.shared = [m.bank[i] for i in turns], shared
        self.masked, self.v, self.out, self.dv, self.wrap = masked, v, out, dv, wrap
        self.km, self.sc, self.pt = bufs
        self.stats = m.small[:, 48:56].rearrange("p (a b) -> p a b", a=2)
        self.sums = m.small[:, 56:64].rearrange("p (a b) -> p a b", a=2)
        self.rc = m.small[:, 40:48].rearrange("p (a b) -> p a b", a=2)
        self.s = m.sems(name, "masked sc_ready least exp turned copied_dve copied_act av_ready inverse out")
        self.arrived = arrived

    def ahead(self, it, u, k):
        return it * self.units + (u + k), it + (u + k) // self.units, (u + k) % self.units

    def last(self, u, k):
        return not self.wrap and u + k >= self.units

    def dve_mask(self, eng, it, u, k):
        if self.last(u, k):
            return
        n, it2, u2 = self.ahead(it, u, k)
        eng.wait_ge(self.s.sc_ready, n * TB - 3 * TB + PRIME)
        eng.wait_ge(self.s.least, n * TB - 3 * TB + PRIME)
        self.masked(eng, self.km[u2 % 4], it2, u2).then_inc(self.s.masked, 1)

    def pe_scores(self, eng, it, u, k, q):
        if self.last(u, k):
            return
        m, s = self.m, self.s
        n, it2, u2 = self.ahead(it, u, k)
        if q == 0:
            eng.wait_ge(s.masked, n + 1)
        eng.wait_ge(s.least, n * TB + q - 1 + PRIME)
        w = self.keys(q)
        eng.matmul(m.bank[q % 2][:, 0:w], self.q(u2 % B, q), self.km[u2 % 4][:, 0:w], start=True,
                   stop=True).then_inc(s.sc_ready, 1)

    def dve_least(self, eng, it, u, k, q):
        if self.last(u, k):
            return
        m, s = self.m, self.s
        n, it2, u2 = self.ahead(it, u, k)
        waits = [(s.sc_ready, n * TB + q + 1 + PRIME)]
        if q == 0:
            waits += [(s.turned, n * TB - TB + PRIME)]
            waits += [(s.exp, n * TB - TB + PRIME)]
            if self.arrived:
                waits += [self.arrived(it2, u2)]
        if isinstance(n, int):
            for sem, value in waits:
                eng.wait_ge(sem, value)
        else:
            held = [(sem, eng.to_reg(value)) for sem, value in waits]
            eng.wait_ge(m.loaded, CONSTS)
            for sem, value in held:
                eng.wait_ge(sem, value)
        w = self.keys(q)
        eng.tensor_tensor_reduce(self.sc[:, u2 % 2, q, 0:w], m.bank[q % 2][:, 0:w], self.extra(it2, u2, q),
                                 1.0, 3e38, ALU.add, ALU.min, self.stats[:, u2 % 2, q:q + 1]).then_inc(s.least, 1)

    def act_exp(self, eng, it, u, k, q):
        if self.last(u, k):
            return
        s = self.s
        n, it2, u2 = self.ahead(it, u, k)
        eng.wait_ge(s.least, n * TB + q + 1 + PRIME)
        if q == 0:
            eng.wait_ge(s.inverse, n - 1 + PRIME)
        w = self.keys(q)
        eng.activation(self.sc[:, u2 % 2, q, 0:w], self.sc[:, u2 % 2, q, 0:w], ACT.Exp, scale=-1.0,
                       bias=self.stats[:, u2 % 2, q:q + 1],
                       accum_out=self.sums[:, u2 % 2, q:q + 1]).then_inc(s.exp, 1)

    def pe_turn(self, eng, it, u, q):
        m, s = self.m, self.s
        n = it * self.units + u
        eng.wait_ge(s.exp, n * TB + q + 1 + PRIME)
        sem, value = self.copied(n, q)
        eng.wait_ge(sem, value - len(self.turns) // (2 if self.shared else 1))
        for k in range(self.keys(q) // P):
            last = eng.transpose(self.turns[q % len(self.turns)][:, k * P:k * P + P], self.sc[:, u % 2, q, k * P:k * P + P],
                                 m.mat("ident"))
        last.then_inc(s.turned, 1)

    def copied(self, n, q):
        if self.shared:
            return (self.s.copied_dve, self.s.copied_act)[q % 2], n * (TB // 2) + q // 2 + 1 + PRIME
        return self.s.copied_dve, n * TB + q + 1 + PRIME

    def copy(self, eng, it, u, q):
        m, s = self.m, self.s
        n = it * self.units + u
        eng.wait_ge(s.turned, n * TB + q + 1 + PRIME)
        if q < 2:
            eng.wait_ge(s.av_ready, n - 1 + PRIME)
        w = self.keys(q)
        dst, src = self.pt[:, u % 2, q, 0:w], self.turns[q % len(self.turns)][:, 0:w]
        if self.shared and q % 2:
            eng.activation(dst, src, ACT.Copy).then_inc(s.copied_act, 1)
        else:
            eng.tensor_copy(dst, src).then_inc(s.copied_dve, 1)

    def pe_av(self, eng, it, u, q):
        m, s = self.m, self.s
        n = it * self.units + u
        eng.wait_ge(*self.copied(n, q))
        if q == 0:
            eng.wait_ge(s.out, n - 1 + PRIME)
        nk = self.keys(q) // P
        for k in range(nk):
            last = eng.matmul(m.bank[4 + u % 2][:, q * self.dv:(q + 1) * self.dv],
                              self.pt[:, u % 2, q, k * P:k * P + P], self.v(it, u, k), start=(k == 0),
                              stop=(k == nk - 1))
        if q == TB - 1:
            last.then_inc(s.av_ready, 1)

    def dve_inverse(self, eng, it, u):
        n, s = it * self.units + u, self.s
        eng.wait_ge(s.exp, n * TB + TB + PRIME)
        eng.wait_ge(s.out, n - 1 + PRIME)
        eng.reciprocal(self.rc[:, u % 2, :], self.sums[:, u % 2, :]).then_inc(s.inverse, 1)

    def dve_out(self, eng, it, u):
        m, s = self.m, self.s
        n = it * self.units + u
        eng.wait_ge(s.inverse, n + 1 + PRIME)
        eng.wait_ge(s.av_ready, n + 1 + PRIME)
        src = m.bank[4 + u % 2][:, 0:TB * self.dv].rearrange("p (t d) -> p t d", t=TB)
        eng.tensor_tensor(self.out(it, u), src,
                          self.rc[:, u % 2, :].unsqueeze(2).to_broadcast([P, TB, self.dv]),
                          ALU.mult).then_inc(s.out, 1)

    def dve_prime(self, eng):
        for sem in (self.s.least, self.s.copied_dve, self.s.inverse, self.s.out):
            eng.sem_inc(sem, PRIME)

    def dve_first(self, eng, it):
        for u in range(3):
            self.dve_mask(eng, it, 0, u)
        for q in range(TB):
            self.dve_least(eng, it, 0, 0, q)
        self.dve_least(eng, it, 0, 1, 0)

    def dve_body(self, eng, it, hook=None):
        for u in range(self.units):
            self.copy(eng, it, u, 0)
            self.dve_least(eng, it, u, 1, 1)
            self.dve_inverse(eng, it, u)
            if not self.shared:
                self.copy(eng, it, u, 1)
            self.dve_mask(eng, it, u, 3)
            self.dve_least(eng, it, u, 1, 2)
            self.copy(eng, it, u, 2)
            self.dve_least(eng, it, u, 1, 3)
            if not self.shared:
                self.copy(eng, it, u, 3)
            self.dve_least(eng, it, u, 2, 0)
            self.dve_out(eng, it, u)
            if hook:
                hook(it, u)

    def act_prime(self, eng):
        eng.sem_inc(self.s.exp, PRIME)
        eng.sem_inc(self.s.copied_act, PRIME)

    def act_first(self, eng, it):
        for q in range(TB):
            self.act_exp(eng, it, 0, 0, q)
        self.act_exp(eng, it, 0, 1, 0)

    def act_body(self, eng, it, hook=None):
        for u in range(self.units):
            for q in range(TB):
                if hook:
                    hook(it, u, q)
                self.act_exp(eng, it, u, 1 + (q + 1) // TB, (q + 1) % TB)
                if self.shared and q % 2 == 0:
                    self.copy(eng, it, u, q + 1)

    def pe_prime(self, eng):
        for sem in (self.s.sc_ready, self.s.turned, self.s.av_ready):
            eng.sem_inc(sem, PRIME)

    def pe_first(self, eng, it):
        for q in range(TB):
            self.pe_scores(eng, it, 0, 0, q)
        self.pe_scores(eng, it, 0, 1, 0)

    def pe_body(self, eng, it, hook=None):
        for u in range(self.units):
            for q in range(TB):
                self.pe_turn(eng, it, u, q)
                if hook:
                    hook(it, u, q)
                early = q == TB - 1 and self.lag == 1
                if early:
                    self.pe_av(eng, it, u, q - 1)
                self.pe_scores(eng, it, u, 1 + (q + 1) // TB, (q + 1) % TB)
                if q >= self.lag and not early:
                    self.pe_av(eng, it, u, q - self.lag)
            for q in range(TB - self.lag, TB):
                self.pe_av(eng, it, u, q)


class Project:

    def __init__(self, m, name, o, ot, weights, bias):
        self.m, self.o, self.ot, self.weights, self.bias = m, o, ot, weights, bias
        self.s = m.sems(name, "turned copied ready added")

    def pe(self, eng, base=0):
        m, s = self.m, self.s
        for b in range(B):
            for j in range(len(self.weights)):
                eng.wait_ge(s.copied, self.count(base, b, j) - 1 + PRIME)
                for q in range(TB):
                    last = eng.transpose(m.bank[6 + self.place(b, j)][:, q * P:q * P + P],
                                         self.o[:, TB * b + q, j * P:j * P + P], m.mat("ident"))
                last.then_inc(s.turned, 1)
        for b in range(B):
            eng.wait_ge(s.copied, self.count(base, b, len(self.weights) - 1) + 1 + PRIME)
            eng.wait_ge(s.added, base + b - 1 + PRIME)
            for q in range(TB):
                t = TB * b + q
                dst = m.bank[4 + b % 2][:, q * P:q * P + P]
                if self.bias:
                    eng.matmul(dst, m.row("ones"), m.row(self.bias), start=True, stop=False)
                for j, w in enumerate(self.weights):
                    last = eng.matmul(dst, self.ot[:, j, t * P:t * P + P], w,
                                      start=(j == 0 and not self.bias), stop=(j == len(self.weights) - 1))
            last.then_inc(s.ready, 1)

    def count(self, base, b, j):
        return (base + b) * len(self.weights) + j

    def place(self, b, j):
        return (b * len(self.weights) + j) % 2

    def act(self, eng, base=0):
        m, s = self.m, self.s
        for b in range(B):
            for j in range(len(self.weights)):
                eng.wait_ge(s.turned, self.count(base, b, j) + 1)
                eng.activation(self.ot[:, j, b * S:b * S + S], m.bank[6 + self.place(b, j)][:, :],
                               ACT.Copy).then_inc(s.copied, 1)

    def dve(self, eng, base=0):
        m, s = self.m, self.s
        for b in range(B):
            eng.wait_ge(s.ready, base + b + 1)
            xs = flat(m.x[:, TB * b:TB * b + TB, :])
            eng.tensor_tensor(xs, m.bank[4 + b % 2][:, :], xs, ALU.add).then_inc(s.added, 1)

    def prime_act(self, eng):
        eng.sem_inc(self.s.copied, PRIME)

    def prime_dve(self, eng):
        eng.sem_inc(self.s.added, PRIME)


class RelativeAttention:

    def __init__(self, m):
        self.m = m
        s = self.s = m.sems("l0a", "const q_ready q_out bias k_ready k_out v_ready v_out p_ready p_out pmask pos_ready "
                                   "pos_out wrote0 wrote1 wrote2 wrote3 read0 read1 read2 read3 zero split")
        self.qu, self.qv, self.k, v, km, self.p_lo, self.p, self.pe_t, ps, pb, sc, pt = \
            m.carve((T,), (T,), (T,), (NT, P), (4, S), (S,), (S,), (S,), (B * TB, S), (2 * TB, S + 1),
                    (2 * TB, S), (2 * TB, S))
        self.qv_parts = m.carve((T,), (T,), of=m.parts)
        self.pm_parts = [m.parts[:, 2 * T + i * S:2 * T + (i + 1) * S] for i in range(2)]
        self.v = v
        self.ps = ps.rearrange("p (b q) n -> p b q n", b=B)
        self.pb = pb.rearrange("p (a q) n -> p a q n", a=2)
        halves = [z.rearrange("p (a q) n -> p a q n", a=2) for z in (sc, pt)]
        self.o = m.xn
        self.norm = Norm(m, m.x, m.xn)
        self.norm2 = Norm(m, m.xn, m.xn2)
        self.turn = Turn(m, self.norm2, [(lambda b: m.xt[:, b * S:b * S + S], "l0_g", "l0_b")])
        reads = [s.read0, s.read1, s.read2, s.read3]

        self.core = Core(
            m, "l0c", B, ([km[:, i, :] for i in range(4)], *halves),
            q=lambda b, q: self.qu[:, b * S + q * P:b * S + q * P + P],
            keys=lambda q: S,
            extra=lambda it, u, q: self.ps[:, u, q, :],
            masked=lambda eng, dst, it, u: eng.tensor_scalar(dst, self.k[:, u * S:u * S + S],
                                                             m.mask[:, 0, ds(it, 1)], None, ALU.mult),
            v=lambda it, u, k: self.v[:, TB * u + k, ds(it * 8, 8)],
            out=lambda it, u: self.o[:, TB * u:TB * u + TB, ds(it * 8, 8)],
            dv=8, wrap=True, turns=(2, 3), shared=False, lag=1,
            arrived=lambda it, u: (reads[u], it * 16 + 16))
        self.project = Project(m, "l0p", self.o, self.qu.rearrange("p (a t) -> p a t", a=1), [m.mat("ao")], "l0_bo")
        self.scratch = m.nc.dram_tensor("shift", (B, S, S + 1), F32).ap()

    def sync(self, eng):
        m, s = self.m, self.s
        eng.wait_ge(m.ln_var, B * self.norm.n + 1)
        eng.dma_start(self.pe_t, m.ins["pe"]).then_inc(s.const, 16)
        wrote = [s.wrote0, s.wrote1, s.wrote2, s.wrote3]
        reads = [s.read0, s.read1, s.read2, s.read3]

        def move(h, b, first):
            eng.wait_ge(s.pos_out, h * NT + TB * b + TB)
            if not first:
                eng.wait_ge(reads[b], h * 16)
            rows = self.scratch[b]
            eng.dma_start(rows.rearrange("(q p) n -> p q n", p=P), self.pb[:, b % 2]).then_inc(wrote[b], 16)
            eng.wait_ge(wrote[b], h * 16 + 16)
            if not first:
                eng.wait_ge(self.core.s.least, h * NT - NT + TB * b + TB + PRIME)
            shifted = rows.rearrange("i n -> (i n)")[S:S + S * S].rearrange("(q p n) -> p q n", p=P, n=S)
            eng.dma_start(self.ps[:, b], shifted).then_inc(reads[b], 16)

        for b in range(B):
            move(0, b, True)
        with eng.Fori(1, H + 1) as h:
            for b in range(B):
                move(h, b, False)
        for b in range(B):
            eng.wait_ge(reads[b], 16 * (H + 1))

    def pool(self, eng):
        self.norm.pool(eng)
        self.norm2.pool(eng)

    def dve(self, eng, ch):
        m, s, core = self.m, self.s, self.core
        self.norm.dve(eng, ch)
        self.norm2.dve(eng, ch)
        core.dve_prime(eng)
        self.project.prime_dve(eng)
        eng.memset(self.pb[:, :, :, 0:1], 0.0).then_inc(s.zero, 1)
        neg = -8.0 ** -0.5
        for i, name in enumerate(("l0_u", "l0_v")):
            last = eng.tensor_scalar(m.small[:, i:i + 1], m.col("l0_bq"), m.col(name), neg, ALU.add, ALU.mult)
        last.then_inc(s.bias, 1)
        eng.wait_ge(s.bias, 1)
        for b in range(B):
            sl = slice(b * S, b * S + S)
            eng.wait_ge(s.q_ready, b + 1)
            eng.tensor_scalar(self.qu[:, sl], m.bank[b % 2][:, :], neg, m.small[:, 0:1], ALU.mult, ALU.add)
            eng.tensor_scalar(self.qv[:, sl], m.bank[b % 2][:, :], neg, m.small[:, 1:2], ALU.mult,
                              ALU.add).then_inc(s.q_out, 1)

        eng.wait_ge(s.q_out, B)
        eng.wait_ge(s.v_out, B)
        split(eng, ch.link, self.qv, m.xt[:, :], *self.qv_parts).then_inc(s.split, 1)
        eng.wait_ge(s.p_out, 1)
        ch.link(eng.tensor_scalar(self.pe_t.bitcast(I32), self.p.bitcast(I32), UPPER, None, ALU.bitwise_and))
        ch.link(eng.tensor_tensor(self.p_lo, self.p, self.pe_t, ALU.subtract))

        def pmask(h, first):
            if not first:
                eng.wait_ge(s.pos_ready, h * NT)
            for dst, src in zip(self.pm_parts, (self.pe_t, self.p_lo)):
                last = eng.tensor_scalar(dst, src, m.mask[:, 0, ds(h, 1)], None, ALU.mult)
            last.then_inc(s.pmask, 1)

        pmask(0, True)
        eng.wait_ge(s.k_out, B)
        pmask(1, False)
        core.dve_first(eng, 0)
        with eng.Fori(0, H) as h:
            core.dve_body(eng, h, lambda it, u: pmask(it + 2, False) if u == B - 1 else None)
        eng.wait_ge(core.s.out, H * B + PRIME)
        self.project.dve(eng)
        eng.wait_ge(self.project.s.added, B + PRIME)
        for read in (s.read0, s.read1, s.read2, s.read3):
            eng.wait_ge(read, 16 * (H + 1))

    def positions(self, eng, h, u, q):
        m, s = self.m, self.s
        n = h * NT + (TB * u + q)
        if u == 0 and q == 0:
            eng.wait_ge(s.pmask, h + 1)
        if not (isinstance(h, int) and u == 0 and q < 2):
            eng.wait_ge(s.pos_out, n - 1)
        at = u * S + q * P
        product(eng, m.bank[6 + q % 2][:, :], [t[:, at:at + P] for t in self.qv_parts],
                self.pm_parts).then_inc(s.pos_ready, 1)

    def pe(self, eng):
        m, s, core = self.m, self.s, self.core
        self.turn.pe(eng)
        core.pe_prime(eng)
        eng.wait_ge(s.const, 16)
        for b in range(B):
            self.turn.wait(eng, b)
            sl = slice(b * S, b * S + S)
            if b >= 2:
                eng.wait_ge(s.q_out, b - 1)
                eng.wait_ge(s.k_out, b - 1)
                eng.wait_ge(s.v_out, b - 1)
            eng.matmul(m.bank[b % 2][:, :], m.mat("aq"), m.xt[:, sl], start=True, stop=True).then_inc(s.q_ready, 1)
            eng.matmul(m.bank[2 + b % 2][:, :], m.mat("ak"), m.xt[:, sl], start=True, stop=True).then_inc(s.k_ready, 1)
            for q in range(TB):
                dst = m.bank[4 + b % 2][:, q * P:q * P + P]
                eng.matmul(dst, m.row("ones"), m.row("l0_bv"), start=True, stop=False)
                last = eng.matmul(dst, m.xt[:, b * S + q * P:b * S + q * P + P], m.mat("av"), start=False, stop=True)
            last.then_inc(s.v_ready, 1)
        eng.wait_ge(s.q_out, B - 1)
        eng.matmul(m.bank[0][:, :], m.mat("ap"), self.pe_t, start=True, stop=True).then_inc(s.p_ready, 1)
        eng.wait_ge(s.q_out, B)
        eng.wait_ge(s.v_out, B)
        eng.wait_ge(s.split, 1)
        for u in range(B):
            for q in range(TB):
                self.positions(eng, 0, u, q)
        eng.wait_ge(s.p_out, 1)
        core.pe_first(eng, 0)
        with eng.Fori(0, H) as h:
            core.pe_body(eng, h, lambda it, u, q: self.positions(eng, it + 1, u, q))
        eng.wait_ge(core.s.out, H * B + PRIME)
        eng.wait_ge(core.s.least, H * NT + TB + 1 + PRIME)
        eng.wait_ge(s.pos_out, (H + 1) * NT)
        self.project.pe(eng)

    def act(self, eng):
        m, s, core = self.m, self.s, self.core
        self.turn.act(eng)
        core.act_prime(eng)
        self.project.prime_act(eng)
        for b in range(B):
            sl = slice(b * S, b * S + S)
            eng.wait_ge(s.k_ready, b + 1)
            eng.activation(self.k[:, sl], m.bank[2 + b % 2][:, :], ACT.Identity, bias=m.col("l0_bk")
                           ).then_inc(s.k_out, 1)
            eng.wait_ge(s.v_ready, b + 1)
            eng.activation(flat(self.v[:, TB * b:TB * b + TB, :]), m.bank[4 + b % 2][:, :], ACT.Copy
                           ).then_inc(s.v_out, 1)
        eng.wait_ge(s.p_ready, 1)
        eng.activation(self.p, m.bank[0][:, :], ACT.Copy).then_inc(s.p_out, 1)
        wrote = [s.wrote0, s.wrote1, s.wrote2, s.wrote3]
        eng.wait_ge(s.zero, 1)

        def copies(h, u, q, first=False):
            n = h * NT + (TB * u + q)
            if q == 0 and not (first and u < 2):
                eng.wait_ge(wrote[(u + 2) % B], h * 16 + (16 if u >= 2 else 0))
            eng.wait_ge(s.pos_ready, n + 1)
            eng.activation(self.pb[:, u % 2, q, 1:S + 1], m.bank[6 + q % 2][:, :], ACT.Copy).then_inc(s.pos_out, 1)

        for u in range(B):
            for q in range(TB):
                copies(0, u, q, True)
        core.act_first(eng, 0)
        with eng.Fori(0, H) as h:
            core.act_body(eng, h, lambda it, u, q: copies(it + 1, u, q))
        self.project.act(eng)


class DistanceAttention:

    def __init__(self, m):
        self.m = m
        s = self.s = m.sems("l3a",
            "const q_ready q_out k_ready k_out v_ready v_out absq square "
            "sums row_in row_ready col_ready one_in one_ready fin_in "
            "fin_ready den root")
        self.q, self.k, self.v, km, self.aq, sc, pt, self.one, self.head, self.junk = m.carve(
            (T,), (T,), (NT, P), (4, S), (T,), (2 * TB, S), (2 * TB, S), (P,), (H,), (2, S))
        halves = [z.rearrange("p (a q) n -> p a q n", a=2) for z in (sc, pt)]
        self.o = m.xn2
        self.norm = Norm(m, m.x, m.xn)
        self.turn = Turn(m, self.norm, [(lambda b: m.xt[:, b * S:b * S + S], None, None)])
        self.scale, self.const = m.gates[0], m.gates[1]
        self.own = m.small[:, 0:B]

        def masked(eng, dst, it, u):
            eng.tensor_copy(self.own[:, u:u + 1], self.const[:, ds(it * B + u, 1)])
            return eng.tensor_scalar(dst, self.k[:, u * S:u * S + S], m.mask[:, 0, ds(it, 1)],
                                     self.scale[:, ds(it * B + u, 1)], ALU.mult, ALU.mult)

        self.core = Core(
            m, "l3c", B, ([km[:, i, :] for i in range(4)], *halves),
            q=lambda b, q: self.q[:, b * S + q * P:b * S + q * P + P],
            keys=lambda q: S,
            extra=lambda it, u, q: self.own[:, u:u + 1].to_broadcast([P, S]),
            masked=masked,
            v=lambda it, u, k: self.v[:, TB * u + k, ds(it * 8, 8)],
            out=lambda it, u: self.o[:, TB * u:TB * u + TB, ds(it * 8, 8)],
            dv=8, wrap=True, turns=(2, 3, 6, 7), shared=True, lag=1)
        self.project = Project(m, "l3p", self.o, self.aq.rearrange("p (a t) -> p a t", a=1), [m.mat("po")], "l3_bo")

    def sync(self, eng):
        m, s = self.m, self.s
        eng.wait_ge(m.ln_var, B * self.norm.n + 1)
        eng.dma_start(self.one, m.ins["ones"]).then_inc(s.const, 16)

    def pool(self, eng):
        m, s = self.m, self.s
        self.norm.pool(eng)
        eng.wait_ge(s.den, 1)
        r = m.small
        eng.tensor_tensor(r[0:H, 20:24], r[0:H, 8:12], r[0:H, 16:20], ALU.pow).then_inc(s.root, 1)

    def dve(self, eng, ch):
        m, s, core = self.m, self.s, self.core
        r = m.small
        self.norm.dve(eng, ch)
        core.dve_prime(eng)
        self.project.prime_dve(eng)
        eng.wait_ge(s.const, 16)
        for b in range(B):
            sl = slice(b * S, b * S + S)
            eng.wait_ge(s.q_ready, b + 1)
            eng.tensor_scalar(self.q[:, sl], m.bank[b % 2][:, :], m.col("l3_bq"), None, ALU.add).then_inc(s.q_out, 1)
        eng.wait_ge(s.k_out, B)
        self.turn.wait(eng)
        k3 = self.k.rearrange("p (b n) -> p b n", b=B)
        x3 = m.xt[:, :].rearrange("p (b n) -> p b n", b=B)
        eng.tensor_reduce(r[:, 0:4], k3, AX.X, ALU.add, apply_absolute_value=True)
        eng.tensor_reduce(r[:, 4:8], x3, AX.X, ALU.add, apply_absolute_value=True).then_inc(s.sums, 1)
        for b in range(B):
            eng.wait_ge(s.row_ready, b + 1)
            eng.tensor_reduce(r[0:H, 12 + b:13 + b], m.bank[b][0:H, :], AX.X, ALU.max).then_inc(s.row_in, 1)
        eng.wait_ge(s.col_ready, 1)
        eng.tensor_reduce(self.head[0:B, :], m.bank[4][0:B, 0:P].rearrange("p (h d) -> p h d", h=H), AX.X, ALU.max)
        ch.link(eng.tensor_reduce(r[0:B, 24:25], m.bank[4][0:B, P:2 * P], AX.X, ALU.max))
        ch.link(eng.tensor_scalar(self.junk[0:B, 0, 0:B], m.mat("ident")[0:B, 0:B], r[0:B, 24:25], None, ALU.mult))
        eng.sem_inc(s.one_in, 1)
        eng.wait_ge(s.one_ready, 1)
        kc, inf, fro = r[0:H, 28:32], r[0:H, 32:36], r[0:H, 8:12]
        eng.memset(r[0:H, 16:20], 0.5)
        eng.tensor_copy(kc, m.bank[5][0:H, 0:B])
        eng.tensor_copy(inf, m.bank[5][0:H, B:2 * B])
        ch.link(eng.tensor_copy(fro, m.bank[5][0:H, 2 * B:3 * B]))
        eng.sem_inc(s.den, 1)
        eng.wait_ge(s.root, 1)
        eng.wait_ge(s.row_in, B)
        row, root = r[0:H, 12:16], r[0:H, 20:24]
        ch.link(eng.tensor_tensor(root, root, inf, ALU.mult))
        ch.link(eng.reciprocal(inf, root))
        ch.link(eng.tensor_tensor(row, row, row, ALU.mult))
        ch.link(eng.tensor_tensor(kc, kc, kc, ALU.mult))
        ch.link(eng.tensor_tensor(row, row, kc, ALU.add))
        ch.link(eng.tensor_tensor(row, row, inf, ALU.mult))
        ch.link(eng.tensor_scalar(inf, inf, -2.0, None, ALU.mult))
        for i, v in enumerate((inf, row)):
            d = self.junk[0:H, i, 0:H * B].rearrange("p (h b) -> p h b", b=B)
            last = eng.tensor_tensor(d, m.mat("ident")[0:H, 0:H].unsqueeze(2).to_broadcast([H, H, B]),
                                     v.unsqueeze(1).to_broadcast([H, H, B]), ALU.mult)
        ch.link(last)
        eng.sem_inc(s.fin_in, 1)
        eng.memset(self.scale[:, :], 0.0)
        ch.link(eng.memset(self.const[:, :], 0.0))
        eng.wait_ge(s.fin_ready, 1)
        eng.tensor_copy(self.scale[:, 0:H * B], m.bank[4][:, 0:H * B])
        ch.link(eng.tensor_copy(self.const[:, 0:H * B], m.bank[4][:, H * B:2 * H * B]))
        core.dve_first(eng, 0)
        with eng.Fori(0, H) as h:
            core.dve_body(eng, h)
        eng.wait_ge(core.s.out, H * B + PRIME)
        self.project.dve(eng)
        eng.wait_ge(self.project.s.added, B + PRIME)

    def pe(self, eng):
        m, s, core = self.m, self.s, self.core
        r = m.small
        self.turn.pe(eng)
        core.pe_prime(eng)
        for b in range(B):
            self.turn.wait(eng, b)
            sl = slice(b * S, b * S + S)
            if b >= 2:
                eng.wait_ge(s.q_out, b - 1)
                eng.wait_ge(s.k_out, b - 1)
                eng.wait_ge(s.v_out, b - 1)
            eng.matmul(m.bank[b % 2][:, :], m.mat("pq"), m.xt[:, sl], start=True, stop=True).then_inc(s.q_ready, 1)
            eng.matmul(m.bank[2 + b % 2][:, :], m.mat("pk"), m.xt[:, sl], start=True, stop=True).then_inc(s.k_ready, 1)
            for q in range(TB):
                dst = m.bank[4 + b % 2][:, q * P:q * P + P]
                eng.matmul(dst, m.row("ones"), m.row("l3_bv"), start=True, stop=False)
                last = eng.matmul(dst, m.xt[:, b * S + q * P:b * S + q * P + P], m.mat("pv"), start=False, stop=True)
            last.then_inc(s.v_ready, 1)
        eng.wait_ge(s.const, 16)
        eng.wait_ge(s.q_out, B)
        eng.wait_ge(s.v_out, B)
        eng.wait_ge(s.k_out, B)
        for b in range(B):
            eng.wait_ge(s.absq, b + 1)
            eng.matmul(m.bank[b][0:H, :], m.mask[:, 0, 0:H], self.aq[:, b * S:b * S + S], start=True,
                       stop=True).then_inc(s.row_ready, 1)
        eng.wait_ge(s.sums, 1)
        eng.transpose(m.bank[4][0:B, 0:P], r[:, 0:4], m.mat("ident"))
        eng.transpose(m.bank[4][0:B, P:2 * P], r[:, 4:8], m.mat("ident")).then_inc(s.col_ready, 1)
        eng.wait_ge(s.one_in, 1)
        eng.wait_ge(s.square, B)
        eng.transpose(m.bank[5][0:H, 0:B], self.head[0:B, :], m.mat("ident")[0:B, 0:B])
        eng.matmul(m.bank[5][0:H, B:2 * B], self.one[0:B, 0:H], self.junk[0:B, 0, 0:B], start=True, stop=True)
        eng.matmul(m.bank[5][0:H, 2 * B:3 * B], m.mask[:, 0, 0:H], r[:, 36:40], start=True,
                   stop=True).then_inc(s.one_ready, 1)
        eng.wait_ge(s.fin_in, 1)
        for i in range(2):
            last = eng.matmul(m.bank[4][:, i * H * B:(i + 1) * H * B], self.one[0:H, :], self.junk[0:H, i, 0:H * B],
                              start=True, stop=True)
        last.then_inc(s.fin_ready, 1)
        eng.wait_ge(s.row_in, B)
        core.pe_first(eng, 0)
        with eng.Fori(0, H) as h:
            core.pe_body(eng, h)
        eng.wait_ge(core.s.out, H * B + PRIME)
        eng.wait_ge(core.s.least, H * NT + TB + 1 + PRIME)
        self.project.pe(eng)

    def act(self, eng):
        m, s, core = self.m, self.s, self.core
        self.turn.act(eng)
        core.act_prime(eng)
        self.project.prime_act(eng)
        for b in range(B):
            sl = slice(b * S, b * S + S)
            eng.wait_ge(s.k_ready, b + 1)
            eng.activation(self.k[:, sl], m.bank[2 + b % 2][:, :], ACT.Identity, bias=m.col("l3_bk")
                           ).then_inc(s.k_out, 1)
            eng.wait_ge(s.v_ready, b + 1)
            eng.activation(flat(self.v[:, TB * b:TB * b + TB, :]), m.bank[4 + b % 2][:, :], ACT.Copy
                           ).then_inc(s.v_out, 1)
        for b in range(B):
            sl = slice(b * S, b * S + S)
            eng.wait_ge(s.q_out, b + 1)
            eng.activation(self.aq[:, sl], self.q[:, sl], ACT.Abs).then_inc(s.absq, 1)
            if b:
                eng.wait_ge(s.square, b)
            eng.activation(self.junk[:, 1, :], self.q[:, sl], ACT.Square,
                           accum_out=m.small[:, 36 + b:37 + b]).then_inc(s.square, 1)
        core.act_first(eng, 0)
        with eng.Fori(0, H) as h:
            core.act_body(eng, h)
        self.project.act(eng)


class RotaryAttention:

    HPS = H // 2
    WIDE = 5 * P + 4

    def __init__(self, m):
        self.m = m
        s = self.s = m.sems("l1a", "const bo_ready bo_added w_in wo_in both_ready half rope v_ready v_out")
        self.q, self.k, self.v, km, sc, pt, self.w, self.wo, tabs, self.causal, self.t, ot = m.carve(
            (T,), (T,), (NT, P), (4, S), (2 * TB, S), (2 * TB, S), (self.WIDE,), (P,), (4, S), (S,), (4, S), (T,))
        self.tabs = tabs
        halves = [z.rearrange("p (a q) n -> p a q n", a=2) for z in (sc, pt)]
        self.o = m.xn
        self.norm = Norm(m, m.x, m.xn)
        self.turn = Turn(m, self.norm, [(lambda b: m.xt[:, b * S:b * S + S], None, None)])
        self.core = Core(
            m, "l1c", 2 * B, ([km[:, i, :] for i in range(4)], *halves),
            q=lambda b, q: self.q[:, b * S + q * P:b * S + q * P + P],
            keys=lambda q: (q + 1) * P,
            extra=lambda it, u, q: self.causal[:, (TB - 1 - q) * P:S],
            masked=lambda eng, dst, it, u: eng.tensor_scalar(dst, self.k[:, u % B * S:u % B * S + S],
                                                             m.mask2[:, u // B:u // B + 1], None, ALU.mult),
            v=lambda it, u, k: self.v[:, TB * (u % B) + k, u // B * 64:u // B * 64 + 64],
            out=lambda it, u: self.o[:, TB * (u % B):TB * (u % B) + TB, u // B * 64:u // B * 64 + 64],
            dv=64, wrap=False, turns=(2, 3, 6, 7), shared=False, lag=2)
        self.project = Project(m, "l1p", self.o, ot.rearrange("p (a t) -> p a t", a=1), [self.wo], None)

    def sync(self, eng):
        m, s = self.m, self.s
        eng.wait_ge(m.ln_var, B * self.norm.n + 1)
        eng.dma_start(self.tabs, m.ins["rotary"]).then_inc(s.const, 16)
        eng.dma_start(self.causal, m.ins["causal"]).then_inc(s.const, 16)
        eng.dma_start(self.w, m.ins["l1_qkv"][0]).then_inc(s.w_in, 16)
        eng.dma_start(self.wo, m.ins["l1_wo"][0]).then_inc(s.wo_in, 16)
        with eng.Fori(1, self.HPS) as i:
            eng.wait_ge(s.v_ready, i * B)
            eng.wait_ge(s.rope, i * (2 * B) + PRIME)
            eng.dma_start(self.w, m.ins["l1_qkv"][ds(i, 1)].rearrange("e p n -> p (e n)")).then_inc(s.w_in, 16)
            eng.wait_ge(self.project.s.ready, i * B)
            eng.dma_start(self.wo, m.ins["l1_wo"][ds(i, 1)].rearrange("e p n -> p (e n)")).then_inc(s.wo_in, 16)

    def pool(self, eng):
        self.norm.pool(eng)

    def dve(self, eng, ch):
        m, s, core = self.m, self.s, self.core
        self.norm.dve(eng, ch)
        core.dve_prime(eng)
        self.project.prime_dve(eng)
        eng.sem_inc(s.rope, PRIME)
        eng.wait_ge(s.const, 32)
        eng.wait_ge(s.bo_ready, 1)
        ch.link(eng.tensor_tensor(m.x[:, :, :], m.x[:, :, :],
                                  m.bank[4][:, 0:P].unsqueeze(1).to_broadcast([P, NT, P]), ALU.add))
        eng.sem_inc(s.bo_added, 1)
        with eng.Fori(0, self.HPS) as hp:
            for part in range(2):
                for b in range(B):
                    n = hp * (2 * B) + (part * B + b)
                    a, c = self.t[:, 2 * (b % 2), :], self.t[:, 2 * (b % 2) + 1, :]
                    eng.wait_ge(s.both_ready, n + 1)
                    eng.wait_ge(s.rope, n - 1 + PRIME)
                    col = 5 * P + 2 * part
                    eng.scalar_tensor_tensor(out=a, in0=m.bank[b % 2][:, :], scalar=self.w[:, col:col + 1],
                                             in1=self.tabs[:, 2 * part, :], op0=ALU.add, op1=ALU.mult)
                    eng.scalar_tensor_tensor(out=c, in0=m.bank[2 + b % 2][:, :], scalar=self.w[:, col + 1:col + 2],
                                             in1=self.tabs[:, 2 * part + 1, :], op0=ALU.add,
                                             op1=ALU.mult).then_inc(s.half, 1)
                    eng.wait_ge(s.half, n + 1)
                    dst = [self.q, self.k][part][:, b * S:b * S + S]
                    eng.tensor_tensor(dst, a, c, ALU.add).then_inc(s.rope, 1)
            eng.wait_ge(s.rope, hp * (2 * B) + 2 * B + PRIME)
            core.dve_first(eng, hp)
            core.dve_body(eng, hp)
            self.project.dve(eng, hp * B)
        eng.wait_ge(self.project.s.added, self.HPS * B + PRIME)

    def pe(self, eng):
        m, s, core = self.m, self.s, self.core
        self.turn.pe(eng)
        core.pe_prime(eng)
        self.turn.wait(eng)
        eng.matmul(m.bank[4][:, 0:P], m.row("ones"), m.row("l1_bo"), start=True, stop=True).then_inc(s.bo_ready, 1)
        eng.wait_ge(s.bo_added, 1)
        with eng.Fori(0, self.HPS) as hp:
            eng.wait_ge(s.w_in, hp * 16 + 16)
            for part in range(2):
                for b in range(B):
                    n = hp * (2 * B) + (part * B + b)
                    eng.wait_ge(s.rope, n - 1 + PRIME)
                    for i in range(2):
                        w = self.w[:, (2 * part + i) * P:(2 * part + i + 1) * P]
                        last = eng.matmul(m.bank[2 * i + b % 2][:, :], w, m.xt[:, b * S:b * S + S], start=True,
                                          stop=True)
                    last.then_inc(s.both_ready, 1)
            for b in range(B):
                eng.wait_ge(self.project.s.added, hp * B + PRIME)
                eng.wait_ge(s.v_out, hp * B + (b - 1) + PRIME)
                for q in range(TB):
                    dst = m.bank[4 + b % 2][:, q * P:q * P + P]
                    t = b * S + q * P
                    eng.matmul(dst, m.xt[:, t:t + P], self.w[:, 4 * P:5 * P], start=True, stop=False)
                    last = eng.matmul(dst, m.row("ones"), m.row_at("l1_bv", hp * P, P), start=False, stop=True)
                last.then_inc(s.v_ready, 1)
            eng.wait_ge(s.v_out, hp * B + B + PRIME)
            core.pe_first(eng, hp)
            core.pe_body(eng, hp)
            eng.wait_ge(core.s.out, hp * (2 * B) + 2 * B + PRIME)
            eng.wait_ge(s.wo_in, hp * 16 + 16)
            self.project.pe(eng, hp * B)

    def act(self, eng):
        m, s, core = self.m, self.s, self.core
        self.turn.act(eng)
        core.act_prime(eng)
        self.project.prime_act(eng)
        eng.sem_inc(s.v_out, PRIME)
        with eng.Fori(0, self.HPS) as hp:
            for b in range(B):
                eng.wait_ge(s.v_ready, hp * B + b + 1)
                eng.activation(flat(self.v[:, TB * b:TB * b + TB, :]), m.bank[4 + b % 2][:, :], ACT.Copy
                               ).then_inc(s.v_out, 1)
            core.act_first(eng, hp)
            core.act_body(eng, hp)
            self.project.act(eng, hp * B)


class LinearCore:

    BANKS = (0, 1, 6, 7)

    def __init__(self, m, name, half, qm, pt, q, k, va, table, o):
        self.m, self.half, self.qm, self.pt, self.q, self.k, self.va = m, half, qm, pt, q, k, va
        self.table, self.o = table, o
        self.s = m.sems(name, "masked sc_ready weighed av_ready sum inverse out")
        self.sums = m.small[:, 48:56].rearrange("p (a b) -> p a b", a=2)
        self.rc = m.small[:, 56:64].rearrange("p (a b) -> p a b", a=2)

    def dve_mask(self, eng, it, u, k):
        n, it2, u2 = it * B + (u + k), it + (u + k) // B, (u + k) % B
        eng.wait_ge(self.s.sc_ready, n * TB - 3 * TB + PRIME)
        eng.tensor_scalar(self.qm[:, u2, :], self.q[:, self.half, u2 * S:u2 * S + S],
                          self.m.mask[:, 1, ds(it2, 1)], None, ALU.mult).then_inc(self.s.masked, 1)

    def pe_scores(self, eng, it, u, k, t):
        n, u2 = it * B + (u + k), (u + k) % B
        s, m = self.s, self.m
        if t == 0:
            eng.wait_ge(s.masked, n + 1)
        eng.wait_ge(s.weighed, n * TB + t - 3 + PRIME)
        at = u2 * S + t * P
        eng.matmul(m.bank[self.BANKS[t]][:, 0:S - t * P], self.k[:, self.half, at:at + P], self.qm[:, u2, t * P:S],
                   start=True, stop=True).then_inc(s.sc_ready, 1)

    def dve_weigh(self, eng, it, u, k, t):
        n, it2, u2 = it * B + (u + k), it + (u + k) // B, (u + k) % B
        s, m = self.s, self.m
        eng.wait_ge(s.sc_ready, n * TB + t + 1 + PRIME)
        if t == 0:
            eng.wait_ge(s.av_ready, n - 1 + PRIME)
        eng.tensor_tensor(self.pt[:, u2 % 2, t, t * P:S], m.bank[self.BANKS[t]][:, 0:S - t * P],
                          self.table(it2)[:, 0:S - t * P], ALU.mult).then_inc(s.weighed, 1)

    def pe_av(self, eng, it, u):
        n = it * B + u
        s, m = self.s, self.m
        eng.wait_ge(s.out, n - 1 + PRIME)
        eng.wait_ge(s.weighed, n * TB + TB + PRIME)
        for q in range(TB):
            for t in range(q + 1):
                last = eng.matmul(m.bank[2 + u % 2][:, q * 17:q * 17 + 17], self.pt[:, u % 2, t, q * P:q * P + P],
                                  self.va[:, TB * u + t, ds((it + 8 * self.half) * 17, 17)], start=(t == 0),
                                  stop=(t == q))
        last.then_inc(s.av_ready, 1)

    def dve_out(self, eng, it, u):
        n = it * B + u
        s, m = self.s, self.m
        eng.wait_ge(s.av_ready, n + 1 + PRIME)
        src = m.bank[2 + u % 2][:, 0:TB * 17].rearrange("p (t d) -> p t d", t=TB)
        eng.tensor_scalar(self.sums[:, u % 2, :], src[:, :, 16], 1e-5, None, ALU.add).then_inc(s.sum, 1)
        eng.wait_ge(s.sum, n + 1)
        eng.reciprocal(self.rc[:, u % 2, :], self.sums[:, u % 2, :]).then_inc(s.inverse, 1)
        eng.wait_ge(s.inverse, n + 1)
        eng.tensor_tensor(self.o[:, TB * u:TB * u + TB, ds((it + 8 * self.half) * 16, 16)], src[:, :, 0:16],
                          self.rc[:, u % 2, :].unsqueeze(2).to_broadcast([P, TB, 16]), ALU.mult).then_inc(s.out, 1)

    def dve(self, eng):
        for sem in (self.s.weighed, self.s.out):
            eng.sem_inc(sem, PRIME)
        for u in range(3):
            self.dve_mask(eng, 0, 0, u)
        for t in range(TB):
            self.dve_weigh(eng, 0, 0, 0, t)
        with eng.Fori(0, 8) as it:
            for u in range(B):
                self.dve_mask(eng, it, u, 3)
                for t in range(TB):
                    self.dve_weigh(eng, it, u, 1, t)
                self.dve_out(eng, it, u)
        eng.wait_ge(self.s.masked, 8 * B + 3)
        eng.wait_ge(self.s.weighed, 8 * B * TB + TB + PRIME)
        eng.wait_ge(self.s.out, 8 * B + PRIME)

    def pe(self, eng):
        for sem in (self.s.sc_ready, self.s.av_ready):
            eng.sem_inc(sem, PRIME)
        for t in range(TB):
            self.pe_scores(eng, 0, 0, 0, t)
        with eng.Fori(0, 8) as it:
            for u in range(B):
                for t in range(TB):
                    self.pe_scores(eng, it, u, 1, t)
                self.pe_av(eng, it, u)
        eng.wait_ge(self.s.out, 8 * B + PRIME)
        eng.wait_ge(self.s.weighed, 8 * B * TB + TB + PRIME)


class LinearAttention:

    def __init__(self, m):
        self.m = m
        s = self.s = m.sems("l2a",
            "const v_ready v_out tanh gated in_ready shifted exp ready2 "
            "turned copied scale w_scale smeared gt_turned gt_copied "
            "y_ready y_out norm_out")
        self.xs, self.gate, self.qt, kp, self.kt, self.table, va, self.tmp, self.bc = \
            m.carve((2, T), (NT, 256), (2, T), (2 * B, S + 1), (2, T), (9, S), (NT, H * 17), (4, S), (2, P))
        self.pt = flat(kp)[:, 0:2 * TB * S].rearrange("p (a n) -> p a n", n=S)
        self.xin = m.xt
        qm = self.tmp
        self.kp = kp.rearrange("p (a b) n -> p a b n", a=2)
        self.qm, self.va = qm, va
        self.o = self.xs.rearrange("p a t -> p (a t)").rearrange("p (t d) -> p t d", t=NT)
        self.y = m.xn
        pt4 = self.pt.rearrange("p (a q) n -> p a q n", a=2)
        self.norm = Norm(m, m.x, m.xn)
        self.norm2 = Norm(m, m.xn, m.xn2)
        self.turn = Turn(m, self.norm2, [
            (lambda b: self.xin[:, b * S:b * S + S], "in_w", "in_b"),
            (lambda b: self.xs[:, 0, b * S:b * S + S], "q_w", "q_b"),
            (lambda b: self.xs[:, 1, b * S:b * S + S], "k_w", "k_b")])
        self.cores = [
            LinearCore(m, "l2c0", 0, qm, pt4, self.qt, self.kt, va,
                       lambda it: self.table.rearrange("p a n -> p (a n)")[:, ds(it * S, S)], self.o),
            LinearCore(m, "l2c1", 1, qm, pt4, self.qt, self.kt, va, lambda it: self.table[:, 8, :], self.o)]
        self.out_norm = Norm(m, self.y, m.xn2)

    def sync(self, eng):
        m, s = self.m, self.s
        eng.wait_ge(m.ln_var, B * self.norm.n + 1)
        eng.dma_start(self.table, m.ins["decay"]).then_inc(s.const, 16)
        eng.dma_start(self.bc, m.ins["l2_out_ln"]).then_inc(s.const, 16)

    def pool(self, eng):
        self.norm.pool(eng)
        self.norm2.pool(eng)
        self.out_norm.pool(eng)

    GROUPS = NT // 2

    def dve(self, eng, ch):
        m, s = self.m, self.s
        r = m.small
        self.norm.dve(eng, ch)
        self.norm2.dve(eng, ch)
        eng.wait_ge(s.const, 32)
        eng.wait_ge(s.scale, 1)
        ch.link(eng.reciprocal(r[:, 2:4], r[:, 0:2]))
        ch.link(eng.tensor_scalar(r[:, 4:6], r[:, 4:6], 1.0, None, ALU.add))
        ch.link(eng.reciprocal(r[:, 6:8], r[:, 4:6]))
        ch.link(eng.tensor_scalar(r[:, 8:10], r[:, 6:8], -1.0, 1.0, ALU.mult, ALU.add))
        eng.sem_inc(s.w_scale, 1)
        va4 = self.va.rearrange("p t (h d) -> p t h d", d=17)
        eng.memset(va4[:, :, :, 16:17], 1.0)
        last = eng.memset(self.kp[:, :, :, 0:1], 0.0)
        ch.link(last)
        for t in range(NT):
            eng.wait_ge(s.tanh, t + 1)
            eng.scalar_tensor_tensor(out=self.gate[:, t, :], in0=self.tmp[:, t % 2, 0:256], scalar=1.0,
                                     in1=m.bank[t % 2][:, 256:512], op0=ALU.add, op1=ALU.mult).then_inc(s.gated, 1)
        for g in range(2 * self.GROUPS):
            z = self.tmp[:, g % 2, :].rearrange("p (a d) -> p a d", d=16)
            mx = m.gates[0][:, g % 2 * 32:g % 2 * 32 + 32]
            rc = m.gates[1][:, g % 2 * 32:g % 2 * 32 + 32]
            e = self.tmp[:, 2 + g % 2, :].rearrange("p (a d) -> p a d", d=16)

            def wide(v):
                return v.unsqueeze(2).to_broadcast([P, 32, 16])

            eng.wait_ge(s.in_ready, g + 1)
            src = m.bank[2 + g % 2][:, :].rearrange("p (a d) -> p a d", d=16)
            ch.link(eng.tensor_reduce(mx, src, AX.X, ALU.max))
            eng.tensor_tensor(z, src, wide(mx), ALU.subtract).then_inc(s.shifted, 1)
            if g:
                self.divide(eng, ch, g - 1)
        self.divide(eng, ch, 2 * self.GROUPS - 1)
        eng.wait_ge(s.copied, 2 * self.GROUPS)
        for b in range(B):
            for half in range(2):
                t = self.tmp[:, half, :]
                ch.link(eng.tensor_scalar(t, self.kp[:, half, b, 0:S], r[:, 6 + half:7 + half], None, ALU.mult))
                last = eng.scalar_tensor_tensor(out=self.kt[:, half, b * S:b * S + S], in0=self.kp[:, half, b, 1:S + 1],
                                                scalar=r[:, 8 + half:9 + half], in1=t, op0=ALU.mult, op1=ALU.add)
                ch.link(last)
        eng.sem_inc(s.smeared, 1)
        for core in self.cores:
            core.dve(eng)
        for b in range(B):
            gb = flat(self.gate[:, TB * b:TB * b + TB, :])
            eng.scalar_tensor_tensor(out=gb, in0=gb, scalar=0.5, in1=flat(self.o[:, TB * b:TB * b + TB, :]),
                                     op0=ALU.mult, op1=ALU.mult).then_inc(s.ready2, 1)
        for b in range(B):
            eng.wait_ge(s.y_ready, b + 1)
            last = eng.tensor_copy(flat(self.y[:, TB * b:TB * b + TB, :]), m.bank[4 + b % 2][:, :])
            last.then_inc(s.y_out, 1)
        eng.wait_ge(s.y_out, B)
        self.out_norm.dve(eng, ch)
        y = m.xn2
        wide = self.bc.unsqueeze(2).to_broadcast([P, 2, NT, P])
        ch.link(eng.tensor_tensor(y[:, :, :], y[:, :, :], wide[:, 0], ALU.mult))
        ch.link(eng.tensor_tensor(y[:, :, :], y[:, :, :], wide[:, 1], ALU.add))
        ch.link(eng.tensor_tensor(m.x[:, :, :], m.x[:, :, :], y[:, :, :], ALU.add))

    def divide(self, eng, ch, g):
        m, s = self.m, self.s
        e = self.tmp[:, 2 + g % 2, :].rearrange("p (a d) -> p a d", d=16)
        rc = m.gates[1][:, g % 2 * 32:g % 2 * 32 + 32]
        sm = m.gates[2][:, g % 2 * 32:g % 2 * 32 + 32]
        eng.wait_ge(s.exp, g + 1)
        ch.link(eng.tensor_reduce(sm, e, AX.X, ALU.add))
        ch.link(eng.reciprocal(rc, sm))
        eng.tensor_tensor(e, e, rc.unsqueeze(2).to_broadcast([P, 32, 16]), ALU.mult).then_inc(s.norm_out, 1)

    def pe(self, eng):
        m, s = self.m, self.s
        self.turn.pe(eng)
        self.turn.wait(eng)
        for t in range(NT):
            if t >= 2:
                eng.wait_ge(s.v_out, t - 1)
                eng.wait_ge(s.gated, t - 1)
            eng.matmul(m.bank[t % 2][:, :], self.xin[:, t * P:t * P + P], m.w2[:, 0:512], start=True,
                       stop=True).then_inc(s.v_ready, 1)

        def turn(g):
            eng.wait_ge(s.norm_out, g + 1)
            if g >= 2:
                eng.wait_ge(s.copied, g - 1)
            for half in range(2):
                for a in range(2):
                    src = self.tmp[:, 2 + g % 2, a * 256 + half * P:a * 256 + half * P + P]
                    last = eng.transpose(m.bank[4 + g % 2][:, half * 256 + a * P:half * 256 + a * P + P], src,
                                         m.mat("ident"))
            last.then_inc(s.turned, 1)

        for g in range(2 * self.GROUPS):
            part = g // self.GROUPS
            if g >= 2:
                eng.wait_ge(s.shifted, g - 1)
            for a in range(2):
                t = (g % self.GROUPS) * 2 + a
                dst = m.bank[2 + g % 2][:, a * 256:a * 256 + 256]
                eng.matmul(dst, m.row("ones"), m.row(["l2_bq", "l2_bk"][part]), start=True, stop=False)
                last = eng.matmul(dst, self.xs[:, part, t * P:t * P + P],
                                  m.w2[:, 512 + part * 256:768 + part * 256], start=False, stop=True)
            last.then_inc(s.in_ready, 1)
            if g >= 2:
                turn(g - 2)
        turn(2 * self.GROUPS - 2)
        turn(2 * self.GROUPS - 1)
        eng.wait_ge(s.smeared, 1)
        eng.wait_ge(s.copied, 2 * self.GROUPS)
        for core in self.cores:
            core.pe(eng)
        for b in range(B):
            eng.wait_ge(s.ready2, b + 1)
            for half in range(2):
                n = 2 * b + half
                if n >= 2:
                    eng.wait_ge(s.gt_copied, n - 1)
                for q in range(TB):
                    last = eng.transpose(m.bank[6 + half][:, q * P:q * P + P],
                                         self.gate[:, TB * b + q, half * P:half * P + P], m.mat("ident"))
                last.then_inc(s.gt_turned, 1)
        for b in range(B):
            eng.wait_ge(s.gt_copied, 2 * b + 2)
            if b >= 2:
                eng.wait_ge(s.y_out, b - 1)
            for q in range(TB):
                t = b * S + q * P
                for half in range(2):
                    last = eng.matmul(m.bank[4 + b % 2][:, q * P:q * P + P], self.qt[:, half, t:t + P],
                                      m.mat(["wo0", "wo1"][half]), start=(half == 0), stop=(half == 1))
            last.then_inc(s.y_ready, 1)

    def act(self, eng):
        m, s = self.m, self.s
        r = m.small
        ls = COLS.index("ls0")
        sm = COLS.index("smear0")
        self.turn.act(eng)
        eng.activation(r[:, 0:2], m.cols[:, ls:ls + 2], ACT.Exp)
        eng.activation(r[:, 4:6], m.cols[:, sm:sm + 2], ACT.Exp, scale=-1.0).then_inc(s.scale, 1)
        va4 = self.va.rearrange("p t (h d) -> p t h d", d=17)
        for t in range(NT):
            eng.wait_ge(s.v_ready, t + 1)
            eng.activation(va4[:, t, :, 0:16], m.bank[t % 2][:, 0:256].rearrange("p (h d) -> p h d", d=16),
                           ACT.Copy).then_inc(s.v_out, 1)
            if t >= 2:
                eng.wait_ge(s.gated, t - 1)
            eng.activation(self.tmp[:, t % 2, 0:256], m.bank[t % 2][:, 256:512], ACT.Tanh,
                           scale=0.5).then_inc(s.tanh, 1)
        eng.wait_ge(s.w_scale, 1)

        def copy(g):
            part = g // self.GROUPS
            eng.wait_ge(s.turned, g + 1)
            at = (g % self.GROUPS) * 256
            for half in range(2):
                src = m.bank[4 + g % 2][:, half * 256:half * 256 + 256]
                if part == 0:
                    dst = self.qt[:, half, at:at + 256]
                else:
                    dst = self.kp[:, half, at // S, 1 + at % S:257 + at % S]
                last = eng.activation(dst, src, ACT.Copy, scale=r[:, 2 + half:3 + half])
            last.then_inc(s.copied, 1)

        for g in range(2 * self.GROUPS):
            eng.wait_ge(s.shifted, g + 1)
            if g >= 2:
                copy(g - 2)
            eng.activation(self.tmp[:, 2 + g % 2, :], self.tmp[:, g % 2, :], ACT.Exp).then_inc(s.exp, 1)
        copy(2 * self.GROUPS - 2)
        copy(2 * self.GROUPS - 1)
        for b in range(B):
            for half in range(2):
                eng.wait_ge(s.gt_turned, 2 * b + half + 1)
                eng.activation(self.qt[:, half, b * S:b * S + S], m.bank[6 + half][:, :], ACT.Copy
                               ).then_inc(s.gt_copied, 1)


LAYERS = [
    lambda m: [MixFfn(m, 0), RelativeAttention(m), MixFfn(m, 1)],
    lambda m: [GeluMoe(m, 0), RotaryAttention(m), GeluMoe(m, 1)],
    lambda m: [RoutedMoe(m, 0), LinearAttention(m), RoutedMoe(m, 1)],
    lambda m: [SwigluMoe(m, 0), DistanceAttention(m), SwigluMoe(m, 1)],
]


def layer(m, n, stages, consts, out):
    done = m.sem(f"layer{n}_done")
    step = m.sem(f"layer{n}_dve_step")
    stored = m.sem(f"layer{n}_stored")

    with m.nc.Block() as block:

        @block.sync
        def _(sp):
            if consts:
                consts.sync(sp)
            else:
                sp.wait_ge(m.cleared, n)
            for st in stages:
                st.sync(sp)
            if out is not None:
                sp.wait_ge(done, 1)
                sp.dma_start(out.rearrange("b (t p) d -> p (b t) d", p=P), m.x[:, :, :]).then_inc(stored, 16)
                sp.wait_ge(stored, 16)

        @block.gpsimd
        def _(pool):
            if consts:
                consts.pool(pool)
            else:
                pool.wait_ge(m.cleared, n)
            for st in stages:
                st.pool(pool)

        @block.scalar
        def _(act):
            if consts:
                consts.wait(act)
            else:
                act.wait_ge(m.cleared, n)
            for st in stages:
                st.act(act)

        @block.tensor
        def _(pe):
            if consts:
                consts.wait(pe)
            else:
                pe.wait_ge(m.cleared, n)
            for st in stages:
                st.pe(pe)

        @block.vector
        def _(dve):
            ch = Chain(dve, step)
            if consts:
                dve.wait_ge(m.x_loaded, 16 * B)
            else:
                dve.wait_ge(m.cleared, n)
            for st in stages:
                st.dve(dve, ch)
            dve.sem_inc(done, 1)


def program(nc, ins, out):
    with ExitStack() as ctx:
        m = Machine(ctx, nc, ins, out)
        kept = len(m.taken)
        for n, build in enumerate(LAYERS):
            layer(m, n, build(m), Consts(m) if n == 0 else None, out if n == len(LAYERS) - 1 else None)
            nc.clear_and_free_semaphores(m.taken[kept:])
            m.taken = m.taken[:kept]
            nc.gpsimd.sem_inc(m.cleared, 1)


def packed(inputs):
    f = np.float32
    a = {k: np.asarray(v) for k, v in inputs.items()}
    eye = np.eye(P, dtype=f)
    col = {
        "mu_r": a["L0_ffn_mu_r"], "mu_k": a["L0_ffn_mu_k"], "l0_g": a["L0_attn_ln_g"], "l0_b": a["L0_attn_ln_b"],
        "l0_bq": a["L0_attn_bq"], "l0_bk": a["L0_attn_bk"], "l0_u": a["L0_attn_u_bias"].reshape(-1),
        "l0_v": a["L0_attn_v_bias"].reshape(-1), "in_w": a["L2_attn_in_ln_w"], "in_b": a["L2_attn_in_ln_b"],
        "q_w": a["L2_attn_q_ln_w"], "q_b": a["L2_attn_q_ln_b"], "k_w": a["L2_attn_k_ln_w"],
        "k_b": a["L2_attn_k_ln_b"], "l3_bq": a["L3_attn_b_qkv"][:P], "l3_bk": a["L3_attn_b_qkv"][P:2 * P],
        "l3_s": a["L3_ffn_ln_scale"], "l3_b": a["L3_ffn_ln_bias"],
    }
    for i in range(2):
        col[f"smear{i}"] = np.repeat(a["L2_attn_smear_factor"], 16)[i * P:i * P + P]
        col[f"ls{i}"] = np.repeat(a["L2_attn_log_scale"], 16)[i * P:i * P + P]
    wq = a["L3_attn_W_qkv"]
    mat = {
        "ident": eye, "Wr": a["L0_ffn_W_r"].T, "Wk": a["L0_ffn_W_k"].T, "Wv": a["L0_ffn_W_v"].T,
        "aq": a["L0_attn_Wq"], "ak": a["L0_attn_Wk"], "av": a["L0_attn_Wv"], "ap": a["L0_attn_Wp"],
        "ao": a["L0_attn_Wo"], "pq": wq[:, :P], "pk": wq[:, P:2 * P], "pv": wq[:, 2 * P:], "po": a["L3_attn_W_proj"],
        "wo0": a["L2_attn_W_out"][:P], "wo1": a["L2_attn_W_out"][P:],
    }
    row = {
        "ones": np.ones(P, f), "l0_bv": a["L0_attn_bv"], "l0_bo": a["L0_attn_bo"], "l1_bv": a["L1_attn_bv"],
        "l1_bo": a["L1_attn_bo"], "l2_bq": a["L2_attn_bq"], "l2_bk": a["L2_attn_bk"],
        "l3_bv": a["L3_attn_b_qkv"][2 * P:], "l3_bo": a["L3_attn_b_proj"],
    }
    feat = np.arange(P)
    mask = np.zeros((P, 2, NMASK), f)
    mask[feat, 0, feat // 8] = 1
    mask[feat, 1, feat // 16] = 1
    mask2 = np.zeros((P, 2), f)
    mask2[feat, feat // 64] = 1

    def halves(w):
        return w.reshape(w.shape[0], 2, P, w.shape[2]).transpose(0, 2, 1, 3)

    def perpart(v):
        return v.reshape(v.shape[0], 2, P).transpose(0, 2, 1)

    l1 = np.concatenate([a["L1_ffn_w1"], halves(a["L1_ffn_w2"]).reshape(NE, P, -1),
                         halves(a["L1_ffn_w3"]).reshape(NE, P, -1), perpart(a["L1_ffn_b1"]),
                         perpart(a["L1_ffn_b2"])], axis=2)
    shared = [np.concatenate([a["L2_ffn_sh_gate_w"][:, j * P:j * P + P], a["L2_ffn_sh_up_w"][:, j * P:j * P + P],
                              a["L2_ffn_sh_down_w"][j * P:j * P + P]], axis=1) for j in range(2)]

    def pairs(w):
        return w.reshape(E2 // 2, 2, P, H2).transpose(0, 2, 1, 3).reshape(E2 // 2, P, P)

    l2 = np.concatenate([pairs(a["L2_ffn_gate_w"]), pairs(a["L2_ffn_up_w"]),
                         a["L2_ffn_down_w"].reshape(E2 // 2, P, P)], axis=2)
    l3 = np.concatenate([np.concatenate([a["L3_ffn_sWg"][None], a["L3_ffn_Wg"]]),
                         np.concatenate([a["L3_ffn_sWu"][None], a["L3_ffn_Wu"]]),
                         halves(np.concatenate([a["L3_ffn_sWd"][None], a["L3_ffn_Wd"]])).reshape(NE + 1, P, -1)],
                        axis=2)
    freq = np.exp(np.arange(0, P, 2, dtype=f) * f(-np.log(10000.0) / P)).astype(f)
    ang = (np.arange(S, dtype=f)[:, None] * freq).astype(f)
    pe = np.stack([np.sin(ang), np.cos(ang)], axis=-1).reshape(S, P).T
    theta = (f(10000.0) ** (np.arange(0, 64, 2, dtype=f) / f(64))).astype(f)
    freqs = (np.arange(S, dtype=f)[:, None] * (f(1.0) / theta)[None, :]).astype(f)
    emb = np.concatenate([freqs, freqs], axis=1)
    sign = np.where(np.arange(64) % 2 == 0, -1, 1).astype(f)
    cos, sin = (np.concatenate([v.T, v.T]).astype(f) for v in (np.cos(emb), np.sin(emb) * sign))
    causal = np.zeros((P, S), f)
    causal[:, S - P:] = BIG * np.triu(np.ones((P, P), f), 1)
    swap = np.arange(H * 64) ^ 1
    byhead = [w.reshape(H // 2, P, P).transpose(0, 2, 1) for w in
              (a["L1_attn_wq"], a["L1_attn_wq"][swap], a["L1_attn_wk"], a["L1_attn_wk"][swap], a["L1_attn_wv"])]
    biases = [v.reshape(H // 2, P, 1) for v in
              (a["L1_attn_bq"], a["L1_attn_bq"][swap], a["L1_attn_bk"], a["L1_attn_bk"][swap])]
    gap = (np.arange(S)[None, :] - np.arange(P)[:, None]).astype(f)
    slopes = f(2.0) ** np.linspace(0.0, -8.0, H // 2).astype(f)
    decay = np.stack([np.exp(-(sl * np.maximum(gap, 0)).astype(f)) for sl in slopes] + [np.ones_like(gap)])
    decay = (decay * (gap >= 0)).transpose(1, 0, 2).astype(f)
    got = {
        "rotary": np.stack([cos * f(-0.125), sin * f(-0.125), cos, sin], axis=1), "causal": causal,
        "l1_qkv": np.concatenate(byhead + biases, axis=2),
        "l1_wo": a["L1_attn_wo"].T.reshape(H // 2, P, P), "decay": decay,
        "l2_out_ln": np.broadcast_to(np.stack([a["L2_attn_out_ln_w"], a["L2_attn_out_ln_b"]]), (P, 2, P)),
        "pe": pe, "ones": np.ones((P, P), f),
        "l2_router": a["L2_ffn_router_w"].T,
        "l2_e_bias": np.broadcast_to(a["L2_ffn_e_bias"], (P, NT, E2)),
        "l2_w": np.concatenate([np.stack(shared), l2]),
        "l3_gate_w": a["L3_ffn_gate_w"].T, "l3_w": l3,
        "x": a["L0_attn_x"],
        "mats": np.stack([mat[n] for n in MATS], axis=1),
        "cols": np.stack([col[n] for n in COLS], axis=1),
        "rows": np.concatenate([row[n] for n, _ in ROWS])[None, :],
        "mask": mask, "mask2": mask2,
        "w2": np.concatenate([a["L2_attn_W_in"], a["L2_attn_Wq"], a["L2_attn_Wk"]], axis=1),
        "l1_gate_w": a["L1_ffn_gate_w"],
        "l1_gate_b": np.broadcast_to(a["L1_ffn_gate_b"], (P, NT, NE)),
        "l1_b3": a["L1_ffn_b3"],
        "tri8": np.broadcast_to(np.tril(np.ones((8, 8), f), -1), (P, 8, 8)),
        "l1_w": l1,
    }
    return {k: np.ascontiguousarray(v) for k, v in got.items()}


def kernel(**inputs):
    import concourse.bacc as bacc
    from concourse.bass_utils import run_bass_kernel_spmd

    nc = bacc.Bacc("TRN2", target_bir_lowering=False, num_devices=1)
    arrays = packed(inputs)
    ins = {n: nc.dram_tensor(f"in_{n}", a.shape, mybir.dt.from_np(a.dtype), kind="ExternalInput").ap()
           for n, a in arrays.items()}
    out = nc.dram_tensor("out_x", (B, S, P), F32, kind="ExternalOutput").ap()
    program(nc, ins, out)
    got = run_bass_kernel_spmd(nc, [{f"in_{n}": a for n, a in arrays.items()}], core_ids=[0])
    return got.results[0]["out_x"]
```
